# Optimizing a Trainium2 kernel written in Bass

```python
import numpy as np
import jax
import jax.numpy as jnp

def _softmax(x, axis=-1):
    return jax.nn.softmax(x, axis=axis)

def _gelu(x):
    return jax.nn.gelu(x, approximate=True)

def _silu(x):
    return jax.nn.silu(x)

def _sigmoid(x):
    return jax.nn.sigmoid(x)

def _layernorm(x, axis=-1, eps=1e-05):
    m = jnp.mean(x, axis=axis, keepdims=True)
    v = jnp.var(x, axis=axis, keepdims=True)
    return (x - m) / jnp.sqrt(v + eps)

def _scatter_add(tgt, idx, src, axis=0):
    return tgt.at[idx].add(src)

def _segment_sum(src, seg, n):
    return jax.ops.segment_sum(src, seg, n)
kernel_name = 'mk_gnn_preln_d4_gnn_r64_6c72b9'

def setup_inputs(seed: int=0):
    np.random.seed(seed)
    _w = jnp.asarray

    def _rec_inputs():
        import jax
        import jax.numpy as jnp
        _gk = jax.random.key(seed)
        x = -0.000202 + 1 * jax.random.normal(jax.random.fold_in(_gk, 1), (100000, 128), jnp.float32)
        src = jax.random.randint(jax.random.fold_in(_gk, 2), (25000,), 0, 100000, jnp.int32)
        dst = jnp.minimum((100000 * jax.random.uniform(jax.random.fold_in(_gk, 3), (25000,)) ** 2.0).astype(jnp.int32), 99999)
        _o = jnp.argsort(dst, stable=True)
        src = src[_o]
        dst = dst[_o]
        edge_weight = 0.00176116 + 0.999358 * jax.random.normal(jax.random.fold_in(_gk, 13), (25000,), jnp.float32)
        edge_weight1 = 0.000614103 + 0.999867 * jax.random.normal(jax.random.fold_in(_gk, 14), (25000, 1), jnp.float32)
        return (x, src, dst, edge_weight, edge_weight1)
    x, src, dst, edge_weight, edge_weight1 = _rec_inputs()

    def _L0_gnn_setup():
        import jax, jax.numpy as jnp
        import numpy as np
        N_NODES = 50000
        N_EDGES = 12500

        def sage_conv(x, src, dst, W_l, b_l, W_r, num_nodes):
            msg = x[src]
            agg = jax.ops.segment_sum(msg, dst, num_segments=num_nodes)
            cnt = jax.ops.segment_sum(jnp.ones((src.shape[0],), x.dtype), dst, num_segments=num_nodes)
            agg = agg / jnp.maximum(cnt, 1.0)[:, None]
            return agg @ W_l + b_l + x @ W_r
        key = jax.random.key(seed)
        ks = jax.random.split(key, 8)
        d_in, d_hid, d_out = (128, 256, 128)
        s = lambda k, shape, fan: jax.random.normal(k, shape, jnp.float32) / np.sqrt(fan)
        return {'x': jax.random.normal(ks[0], (N_NODES, d_in), jnp.float32), 'edge_index': jax.random.randint(ks[1], (2, N_EDGES), 0, N_NODES, jnp.int64), 'W1_l': s(ks[2], (d_in, d_hid), d_in), 'b1': jnp.zeros((d_hid,), jnp.float32), 'W1_r': s(ks[3], (d_in, d_hid), d_in), 'W2_l': s(ks[4], (d_hid, d_out), d_hid), 'b2': jnp.zeros((d_out,), jnp.float32), 'W2_r': s(ks[5], (d_hid, d_out), d_hid)}
    _L0_gnn_all = _L0_gnn_setup()
    _L0_gnn_in = {k: v for k, v in _L0_gnn_all.items() if k in ('W1_l', 'b1', 'W1_r', 'W2_l', 'b2', 'W2_r')}
    del _L0_gnn_all

    def _L1_gnn_setup():
        import jax, jax.numpy as jnp
        import numpy as np
        N_NODES = 50000
        N_EDGES = 12500
        IN_DIM = 128
        NUM_HEADS = 8
        HEAD_DIM = IN_DIM // NUM_HEADS
        key = jax.random.key(seed)
        ks = jax.random.split(key, 14)
        return {'x': jax.random.normal(ks[0], (N_NODES, IN_DIM), dtype=jnp.float32), 'expander_edge_index': jax.random.randint(ks[1], (2, N_EDGES), 0, N_NODES, dtype=jnp.int64 if jax.config.jax_enable_x64 else jnp.int32), 'expander_edge_attr': jax.random.normal(ks[2], (N_EDGES, 1), dtype=jnp.float32), 'virt_h': jax.random.normal(ks[3], (1, IN_DIM), dtype=jnp.float32), 'virt_edge_index': jax.random.randint(ks[4], (2, 1), 0, N_NODES, dtype=jnp.int64 if jax.config.jax_enable_x64 else jnp.int32), 'virt_edge_attr': jax.random.normal(ks[5], (1, 1), dtype=jnp.float32), 'Wq': jax.random.normal(ks[6], (IN_DIM, IN_DIM), dtype=jnp.float32) * 0.05, 'bq': jax.random.normal(ks[7], (IN_DIM,), dtype=jnp.float32) * 0.05, 'Wk': jax.random.normal(ks[8], (IN_DIM, IN_DIM), dtype=jnp.float32) * 0.05, 'bk': jax.random.normal(ks[9], (IN_DIM,), dtype=jnp.float32) * 0.05, 'We': jax.random.normal(ks[10], (1, IN_DIM), dtype=jnp.float32) * 0.05, 'be': jax.random.normal(ks[11], (IN_DIM,), dtype=jnp.float32) * 0.05, 'Wv': jax.random.normal(ks[12], (IN_DIM, IN_DIM), dtype=jnp.float32) * 0.05, 'bv': jax.random.normal(ks[13], (IN_DIM,), dtype=jnp.float32) * 0.05}
    _L1_gnn_all = _L1_gnn_setup()
    _L1_gnn_in = {k: v for k, v in _L1_gnn_all.items() if k in ('virt_h', 'virt_edge_index', 'virt_edge_attr', 'Wq', 'bq', 'Wk', 'bk', 'We', 'be', 'Wv', 'bv')}
    del _L1_gnn_all

    def _L2_gnn_setup():
        import jax, jax.numpy as jnp
        import numpy as np
        N_NODES = 100000
        IN_DIM = 128
        OUT_DIM = 128
        N_EDGES = 10000
        BN_EPS = 1e-05

        def _batchnorm(h, gamma, beta):
            mean = jnp.mean(h, axis=0)
            var = jnp.mean(jnp.square(h - mean), axis=0)
            return (h - mean) * jax.lax.rsqrt(var + BN_EPS) * gamma + beta
        key = jax.random.key(seed)
        ks = jax.random.split(key, 8)
        x = jax.random.normal(ks[0], (N_NODES, IN_DIM), dtype=jnp.float32)
        edge_index = jax.random.randint(ks[1], (2, N_EDGES), 0, N_NODES, dtype=jnp.int32)
        s1 = 1.0 / np.sqrt(IN_DIM)
        s2 = 1.0 / np.sqrt(OUT_DIM)
        w1 = jax.random.uniform(ks[2], (IN_DIM, OUT_DIM), minval=-s1, maxval=s1, dtype=jnp.float32)
        b1 = jax.random.uniform(ks[3], (OUT_DIM,), minval=-s1, maxval=s1, dtype=jnp.float32)
        w2 = jax.random.uniform(ks[4], (OUT_DIM, OUT_DIM), minval=-s2, maxval=s2, dtype=jnp.float32)
        b2 = jax.random.uniform(ks[5], (OUT_DIM,), minval=-s2, maxval=s2, dtype=jnp.float32)
        gamma1 = jnp.ones((OUT_DIM,), jnp.float32)
        beta1 = jnp.zeros((OUT_DIM,), jnp.float32)
        gamma2 = jnp.ones((OUT_DIM,), jnp.float32)
        beta2 = jnp.zeros((OUT_DIM,), jnp.float32)
        eps = jnp.zeros((1,), jnp.float32)
        return {'x': x, 'edge_index': edge_index, 'eps': eps, 'w1': w1, 'b1': b1, 'gamma1': gamma1, 'beta1': beta1, 'w2': w2, 'b2': b2, 'gamma2': gamma2, 'beta2': beta2}
    _L2_gnn_all = _L2_gnn_setup()
    _L2_gnn_in = {k: v for k, v in _L2_gnn_all.items() if k in ('eps', 'w1', 'b1', 'gamma1', 'beta1', 'w2', 'b2', 'gamma2', 'beta2')}
    del _L2_gnn_all

    def _L3_gnn_setup():
        import jax, jax.numpy as jnp
        import numpy as np
        N_NODES = 50000
        N_PAIRS = 625000
        F = 128
        key = jax.random.key(seed)
        k1, k2, k3, k4, k5 = jax.random.split(key, 5)
        x = jax.random.normal(k1, (N_NODES, F), dtype=jnp.float32)
        alpha_ij = jax.random.normal(k2, (N_PAIRS,), dtype=jnp.float32)
        idx_i = jax.random.randint(k3, (N_PAIRS,), 0, N_NODES, dtype=jnp.int32)
        idx_j = jax.random.randint(k4, (N_PAIRS,), 0, N_NODES, dtype=jnp.int32)
        W = jax.random.normal(k5, (F, F), dtype=jnp.float32) / np.sqrt(F)
        return {'x': x, 'alpha_ij': alpha_ij, 'idx_i': idx_i, 'idx_j': idx_j, 'W': W}
    _L3_gnn_all = _L3_gnn_setup()
    _L3_gnn_in = {k: v for k, v in _L3_gnn_all.items() if k in ('W',)}
    del _L3_gnn_all
    return {'x': x, 'src': src, 'dst': dst, 'edge_weight': edge_weight, 'edge_weight1': edge_weight1, 'L0_gnn_W1_l': _L0_gnn_in['W1_l'], 'L0_gnn_b1': _L0_gnn_in['b1'], 'L0_gnn_W1_r': _L0_gnn_in['W1_r'], 'L0_gnn_W2_l': _L0_gnn_in['W2_l'], 'L0_gnn_b2': _L0_gnn_in['b2'], 'L0_gnn_W2_r': _L0_gnn_in['W2_r'], 'L1_gnn_virt_h': _L1_gnn_in['virt_h'], 'L1_gnn_virt_edge_index': _L1_gnn_in['virt_edge_index'], 'L1_gnn_virt_edge_attr': _L1_gnn_in['virt_edge_attr'], 'L1_gnn_Wq': _L1_gnn_in['Wq'], 'L1_gnn_bq': _L1_gnn_in['bq'], 'L1_gnn_Wk': _L1_gnn_in['Wk'], 'L1_gnn_bk': _L1_gnn_in['bk'], 'L1_gnn_We': _L1_gnn_in['We'], 'L1_gnn_be': _L1_gnn_in['be'], 'L1_gnn_Wv': _L1_gnn_in['Wv'], 'L1_gnn_bv': _L1_gnn_in['bv'], 'L2_gnn_eps': _L2_gnn_in['eps'], 'L2_gnn_w1': _L2_gnn_in['w1'], 'L2_gnn_b1': _L2_gnn_in['b1'], 'L2_gnn_gamma1': _L2_gnn_in['gamma1'], 'L2_gnn_beta1': _L2_gnn_in['beta1'], 'L2_gnn_w2': _L2_gnn_in['w2'], 'L2_gnn_b2': _L2_gnn_in['b2'], 'L2_gnn_gamma2': _L2_gnn_in['gamma2'], 'L2_gnn_beta2': _L2_gnn_in['beta2'], 'L3_gnn_W': _L3_gnn_in['W']}

def reference(x, src, dst, edge_weight, edge_weight1, L0_gnn_W1_l, L0_gnn_b1, L0_gnn_W1_r, L0_gnn_W2_l, L0_gnn_b2, L0_gnn_W2_r, L1_gnn_virt_h, L1_gnn_virt_edge_index, L1_gnn_virt_edge_attr, L1_gnn_Wq, L1_gnn_bq, L1_gnn_Wk, L1_gnn_bk, L1_gnn_We, L1_gnn_be, L1_gnn_Wv, L1_gnn_bv, L2_gnn_eps, L2_gnn_w1, L2_gnn_b1, L2_gnn_gamma1, L2_gnn_beta1, L2_gnn_w2, L2_gnn_b2, L2_gnn_gamma2, L2_gnn_beta2, L3_gnn_W):
    import jax
    import jax.numpy as jnp

    def _L0_gnn_ref(x, edge_index, W1_l, b1, W1_r, W2_l, b2, W2_r):
        import jax, jax.numpy as jnp
        import numpy as np
        N_NODES = 50000
        N_EDGES = 12500

        def sage_conv(x, src, dst, W_l, b_l, W_r, num_nodes):
            msg = x[src]
            agg = jax.ops.segment_sum(msg, dst, num_segments=num_nodes)
            cnt = jax.ops.segment_sum(jnp.ones((src.shape[0],), x.dtype), dst, num_segments=num_nodes)
            agg = agg / jnp.maximum(cnt, 1.0)[:, None]
            return agg @ W_l + b_l + x @ W_r
        src, dst = (edge_index[0], edge_index[1])
        n = x.shape[0]
        h = sage_conv(x, src, dst, W1_l, b1, W1_r, n)
        h = jax.nn.relu(h)
        out = sage_conv(h, src, dst, W2_l, b2, W2_r, n)
        return out

    def _L1_gnn_ref(x, expander_edge_index, expander_edge_attr, virt_h, virt_edge_index, virt_edge_attr, Wq, bq, Wk, bk, We, be, Wv, bv):
        import jax, jax.numpy as jnp
        import numpy as np
        N_NODES = 50000
        N_EDGES = 12500
        IN_DIM = 128
        NUM_HEADS = 8
        HEAD_DIM = IN_DIM // NUM_HEADS
        N = x.shape[0]
        H, D = (NUM_HEADS, HEAD_DIM)
        Q_h = (x @ Wq + bq).reshape(N, H, D)
        K_h = (x @ Wk + bk).reshape(N, H, D)
        V_h = (x @ Wv + bv).reshape(N, H, D)
        E = (expander_edge_attr @ We + be).reshape(-1, H, D)
        src = expander_edge_index[0]
        dst = expander_edge_index[1]
        score = jnp.sum(K_h[src] * Q_h[dst] * E, axis=-1, keepdims=True) / np.sqrt(D).astype(np.float32)
        score = jnp.exp(jnp.clip(score, -5.0, 5.0))
        msg = V_h[src] * score
        wV = jax.ops.segment_sum(msg, dst, num_segments=N)
        Z = jax.ops.segment_sum(score, dst, num_segments=N)
        h_out = (wV / (Z + 1e-06)).reshape(N, H * D)
        return h_out

    def _L2_gnn_ref(x, edge_index, eps, w1, b1, gamma1, beta1, w2, b2, gamma2, beta2):
        import jax, jax.numpy as jnp
        import numpy as np
        N_NODES = 100000
        IN_DIM = 128
        OUT_DIM = 128
        N_EDGES = 10000
        BN_EPS = 1e-05

        def _batchnorm(h, gamma, beta):
            mean = jnp.mean(h, axis=0)
            var = jnp.mean(jnp.square(h - mean), axis=0)
            return (h - mean) * jax.lax.rsqrt(var + BN_EPS) * gamma + beta
        row, col = (edge_index[0], edge_index[1])
        agg = jax.ops.segment_sum(x[col], row, num_segments=x.shape[0])
        h = (1.0 + eps) * x + agg
        h = jax.nn.relu(_batchnorm(h @ w1 + b1, gamma1, beta1))
        h = jax.nn.relu(_batchnorm(h @ w2 + b2, gamma2, beta2))
        return h

    def _L3_gnn_ref(x, alpha_ij, idx_i, idx_j, W):
        import jax, jax.numpy as jnp
        import numpy as np
        N_NODES = 50000
        N_PAIRS = 625000
        F = 128
        v = jnp.matmul(x, W)
        msg = alpha_ij[:, None] * v[idx_j]
        return jax.ops.segment_sum(msg, segment_ids=idx_i, num_segments=x.shape[0])
    edge_index = jnp.stack([src, dst])
    h = jnp.maximum(_layernorm(x, axis=-1), 0.0)
    x = x + _L0_gnn_ref(h, edge_index, L0_gnn_W1_l, L0_gnn_b1, L0_gnn_W1_r, L0_gnn_W2_l, L0_gnn_b2, L0_gnn_W2_r)
    h = jnp.maximum(_layernorm(x, axis=-1), 0.0)
    x = x + _L1_gnn_ref(h, edge_index, edge_weight1, L1_gnn_virt_h, L1_gnn_virt_edge_index, L1_gnn_virt_edge_attr, L1_gnn_Wq, L1_gnn_bq, L1_gnn_Wk, L1_gnn_bk, L1_gnn_We, L1_gnn_be, L1_gnn_Wv, L1_gnn_bv)
    h = jnp.maximum(_layernorm(x, axis=-1), 0.0)
    x = x + _L2_gnn_ref(h, edge_index, L2_gnn_eps, L2_gnn_w1, L2_gnn_b1, L2_gnn_gamma1, L2_gnn_beta1, L2_gnn_w2, L2_gnn_b2, L2_gnn_gamma2, L2_gnn_beta2)
    h = jnp.maximum(_layernorm(x, axis=-1), 0.0)
    x = x + _L3_gnn_ref(h, edge_weight, src, dst, L3_gnn_W)
    return x

_drawn_inputs = setup_inputs


def setup_inputs(seed=0):
    import zlib

    import numpy as np

    out = dict(_drawn_inputs(seed))
    spreads = {'L0_gnn_b1': (0.0, 0.1),
     'L0_gnn_b2': (0.0, 0.1),
     'L2_gnn_gamma1': (1.0, 0.2),
     'L2_gnn_beta1': (0.0, 0.1),
     'L2_gnn_gamma2': (1.0, 0.2),
     'L2_gnn_beta2': (0.0, 0.1)}
    factors = {'edge_weight1': 8.0,
     'L1_gnn_Wq': 8.0,
     'L1_gnn_bq': 33.96,
     'L1_gnn_Wk': 8.0,
     'L1_gnn_bk': 32.783,
     'L1_gnn_We': 8.0,
     'L1_gnn_be': 22.695,
     'L2_gnn_b1': 64.0,
     'L2_gnn_b2': 64.0}
    for name, (base, spread) in spreads.items():
        noise = np.random.default_rng([zlib.crc32(name.encode()), seed]).standard_normal(out[name].shape)
        drawn = base * np.exp(spread * noise) if base else spread * noise
        out[name] = jnp.asarray(drawn.astype(out[name].dtype))
    for name, factor in factors.items():
        out[name] = (out[name] * factor).astype(out[name].dtype)
    return out
```

```python
import concourse.bass as bass
from concourse import mybir
from contextlib import ExitStack

F = 128
HID = 256
HEADS, HD = 8, 16
J = 2
EPT = 127
UNROLL = 4
ACC_W = 136
LN_EPS = 1e-5
Z_EPS = 1e-6


def begun(s):
    return not isinstance(s, int) or s >= 0


class Signal:

    def __init__(self, sem):
        self.sem, self.base, self.per = sem, 0, 1

    def open(self, per):
        self.per = per
        return self

    def close(self, total):
        self.base += total

    def at(self, s, j=None):
        return self.base + self.per * s + (self.per if j is None else j)

    def next(self):
        self.base += 1
        return self.base


class Slots:

    def __init__(self, sems):
        self.sems, self.base, self.n = sems, [0] * len(sems), 1

    def open(self, n):
        self.n = n
        return self

    def close(self, steps):
        d = len(self.sems)
        for r in range(d):
            self.base[r] += 16 * self.n * ((steps - r + d - 1) // d)

    def sem(self, r):
        return self.sems[r % len(self.sems)]

    def at(self, s, r):
        d = len(self.sems)
        r = r % d
        return self.base[r] + (16 * self.n // d) * (s - r) + 16 * self.n


def steps_at(k, r, lag, n):
    s = k - lag
    if isinstance(s, int) and not 0 <= s < n:
        return []
    return [(s, (r - lag) % UNROLL)]


def drive(eng, total, streams):
    it = 0
    while it < total:
        active = [x for x in streams if x[2][0] <= it < x[2][1]]
        end = total
        for emit, off, (lo, hi), (a, b) in streams:
            if lo <= it < hi:
                end = min(end, hi, b if a <= it < b else it)
            elif it < lo:
                end = min(end, lo)
        m = (end - it) // UNROLL if it % UNROLL == 0 else 0
        if m >= 2 and active:
            with eng.Fori(it // UNROLL, it // UNROLL + m) as i:
                for u in range(UNROLL):
                    for emit, off, _, _ in active:
                        emit(UNROLL * i + (u + off), (u + off) % UNROLL)
            it += m * UNROLL
        else:
            for emit, off, _, _ in active:
                emit(it + off, (it + off) % UNROLL)
            it += 1


def gnn_kernel(nc, N, E, d, out):
    fp32, i32 = mybir.dt.float32, mybir.dt.int32
    ALU, ACT, AX = mybir.AluOpType, mybir.ActivationFunctionType, mybir.AxisListType
    T = -(-E // EPT)
    T += T % J
    NS = T // J
    TH = T // 2
    C = T * 128
    GR = 128 * J
    NF, TAIL = N // GR, (N % GR) // J
    ND = NF + (TAIL > 0)
    J4 = 4
    NF4, TAIL4 = N // (128 * J4), (N % (128 * J4)) // J4
    ND4 = NF4 + (TAIL4 > 0)
    assert N % J4 == 0
    FAR = 1 << 20
    TS = -(-E // 128)
    DIGITS = ((0, 512), (9, 256))
    assert N < DIGITS[1][1] << DIGITS[1][0]
    LEN = d["dst"].shape[0]

    def dram(name, shape, dt=fp32):
        return nc.dram_tensor(name, shape, dt, kind="Internal").ap()

    rep_of = dram("rep_of", [128 * (-(-N // 128)), 1], i32)
    xs_d = dram("xs_d", [C, F])
    a0_d = dram("a0_d", [C + 1, F])
    a1_d = dram("a1_d", [C + 1, F])
    x1s_d = dram("x1s_d", [C, F])
    x1d_d = dram("x1d_d", [C, F])
    qe_d = dram("qe_d", [C, F])
    xyd_d = dram("xyd_d", [C, 2 * F])
    x4_d = dram("x4_d", [C, F])
    x2_d = dram("x2_d", [N, F])
    y_d = dram("y_d", [N, F])
    has_out = dram("has_out", [128 * (-(-N // 128)), 1], i32)
    sorted_d = [dram(f"sorted{i}_d", [128 * TS, 4], i32) for i in range(2)]
    by_src = {n: dram(f"by_src_{n}", [LEN], dt) for n, dt in (("key", i32), ("other", i32), ("w", fp32))}

    def by_step(a):
        return a[0:C, :].rearrange("(q j p) f -> q p j f", j=J, p=128)

    def by_group(a, j):
        full = 128 * j * (N // (128 * j))
        return (a[0:full, :].rearrange("(g p j) f -> g p j f", p=128, j=j),
                a[full:N, :].rearrange("(p j) f -> p j f", j=j) if N > full else None)

    def group(views, s, nfull):
        return views[1] if isinstance(s, int) and s == nfull else views[0][s]

    top = ExitStack()
    with top:
        used_names = {}

        def sb(name, shape, dt=fp32, ctx=top):
            n = used_names[name] = used_names.get(name, 0) + 1
            name = name if n == 1 else f"{name}_{n}"
            return ctx.enter_context(nc.sbuf_tensor(name, shape, dt))

        def sig(name):
            return Signal(top.enter_context(nc.semaphore(name)))

        def slots(name, n=UNROLL):
            return Slots([top.enter_context(nc.semaphore(f"{name}{i}")) for i in range(n)])

        ident = sb("ident", [128, 128])
        w1r = sb("w1r", [128, HID])
        w1l = sb("w1l", [128, HID])
        w2lr = sb("w2lr", [128, 2, 2 * F])
        wq = sb("wq", [128, F])
        wkv = sb("wkv", [128, 2 * F])
        w1 = sb("w1", [128, F])
        w2 = sb("w2", [128, F])
        w3 = sb("w3", [128, F])
        b1 = sb("b1", [128, 2])
        b2 = sb("b2", [128, F])
        bq = sb("bq", [128, F])
        bkv = sb("bkv", [128, 2 * F])
        we = sb("we", [128, F])
        be = sb("be", [128, F])
        cols = sb("cols", [128, 8])
        row_i = sb("row_i", [128, T], i32)
        ss_i = sb("ss_i", [128, T], i32)

        class Tables:

            def __init__(self, tag):
                self.key_p = sb(f"key_p_{tag}", [128, T])
                self.is_rep = sb(f"is_rep_{tag}", [128, T])
                self.key_r = sb(f"key_r_{tag}", [128, T])
                self.rep_r = sb(f"rep_r_{tag}", [128, T])
                self.w = sb(f"w_{tag}", [128, T])
                self.other = sb(f"other_{tag}", [128, T], i32)
                self.key_g = sb(f"key_g_{tag}", [128, T], i32)
                self.key_s = sb(f"key_s_{tag}", [128, T], i32)

        by_d, by_s = Tables("by_dst"), Tables("by_src")
        rcnt = sb("rcnt", [128, T])
        no_out = sb("no_out", [128, J * ND])
        ystat_mem = sb("ystat_mem", [128, max((ND + NS) * 6, 4 * J4 * F)])
        ystat = ystat_mem[:, 0:(ND + NS) * 6].rearrange("p (a c) -> p a c", c=6)
        x3_rows = ystat_mem[:, 0:4 * J4 * F].rearrange("p (b j f) -> p b j f", b=4, j=J4)
        ystat2 = ystat
        bn = sb("bn", [128, 4])
        tiny = sb("tiny", [128, 8])
        ln_eps = sb("ln_eps", [128, 1])

        bank = [top.enter_context(nc.psum_tensor(f"bank{i}", [128, 512], fp32)) for i in range(8)]

        pool_fence = top.enter_context(nc.semaphore("pool_fence"))
        sp_fence = top.enter_context(nc.semaphore("sp_fence"))
        dve_fence = top.enter_context(nc.semaphore("dve_fence"))
        loaded = sig("loaded")
        made = sig("made")
        setup_t = sig("setup_t")
        setup_c = sig("setup_c")
        setup_dma = sig("setup_dma")

        loads = [
            (w1r[:, :], d["L0_gnn_W1_r"]), (w1l[:, :], d["L0_gnn_W1_l"]),
            (w2lr[:, :, 0:F], d["L0_gnn_W2_l"].rearrange("(m k) n -> k m n", m=2)),
            (w2lr[:, :, F:2 * F], d["L0_gnn_W2_r"].rearrange("(m k) n -> k m n", m=2)),
            (wq[:, :], d["L1_gnn_Wq"]), (wkv[:, 0:F], d["L1_gnn_Wk"]), (wkv[:, F:2 * F], d["L1_gnn_Wv"]),
            (w1[:, :], d["L2_gnn_w1"]), (w2[:, :], d["L2_gnn_w2"]), (w3[:, :], d["L3_gnn_W"]),
            (b1[:, 0:1], d["L0_gnn_b1"][0:128].rearrange("(k a) -> k a", a=1)),
            (b1[:, 1:2], d["L0_gnn_b1"][128:HID].rearrange("(k a) -> k a", a=1)),
            (b2[:, :], d["L0_gnn_b2"].partition_broadcast(128)),
            (bq[:, :], d["L1_gnn_bq"].partition_broadcast(128)),
            (bkv[:, 0:F], d["L1_gnn_bk"].partition_broadcast(128)),
            (bkv[:, F:2 * F], d["L1_gnn_bv"].partition_broadcast(128)),
            (we[:, :], d["L1_gnn_We"].rearrange("a f -> (a f)").partition_broadcast(128)),
            (be[:, :], d["L1_gnn_be"].partition_broadcast(128)),
            (cols[:, 6:7], d["L2_gnn_eps"].partition_broadcast(128)),
        ] + [(cols[:, i:i + 1], d[n].rearrange("(k a) -> k a", a=1)) for i, n in enumerate(
            ["L2_gnn_b1", "L2_gnn_gamma1", "L2_gnn_beta1", "L2_gnn_b2", "L2_gnn_gamma2", "L2_gnn_beta2"])]
        NCOL = -(-N // 128)
        with ExitStack() as ph:
            fill = sb("fill", [128, NCOL], i32, ph)
            zero_row = sb("zero_row", [1, F], fp32, ph)
            ends = sb("ends", [1, 3, LEN - TS * 128], i32, ph)
            with nc.Block() as block:
                @block.sync
                def _(sp):
                    for dest, source in loads:
                        sp.dma_start(dest, source).then_inc(loaded.sem, 16)
                    sp.wait_ge(made.sem, 7)
                    n = 0
                    for a in (rep_of, has_out):
                        sp.dma_start(a.rearrange("(p n) a -> p (n a)", p=128), fill[:, :]).then_inc(setup_dma.sem, 16)
                    for a in (a0_d, a1_d):
                        sp.dma_start(a[C:C + 1, :], zero_row[:, :]).then_inc(setup_dma.sem, 16)
                    rest = LEN - 1 - TS * 128
                    for name, i in (("key", 0), ("other", 2), ("w", 2)):
                        a = by_src[name] if name != "w" else by_src[name].bitcast(i32)
                        sp.dma_start(a[0:1].rearrange("(a n) -> a n", a=1), ends[:, i, 0:1]).then_inc(setup_dma.sem, 16)
                        n += 1
                        if rest:
                            sp.dma_start(a[1 + TS * 128:LEN].rearrange("(a n) -> a n", a=1),
                                         ends[:, 1 if name == "key" else 2, 0:rest]).then_inc(setup_dma.sem, 16)
                            n += 1
                    sp.wait_ge(setup_dma.sem, 16 * (4 + n))
                    setup_dma.base = 16 * (4 + n)
                    sp.wait_ge(loaded.sem, 16 * len(loads))

                @block.gpsimd
                def _(pool):
                    pool.memset(ident[:, :], 0.0).then_inc(made.sem, 1)
                    pool.memset(zero_row[:, :], 0.0).then_inc(made.sem, 1)
                    pool.memset(ln_eps[:, :], LN_EPS)
                    pool.iota(ends[:, 0, :], pattern=[[0, LEN - TS * 128]], base=-1, channel_multiplier=0) \
                        .then_inc(made.sem, 1)
                    pool.iota(ends[:, 1, :], pattern=[[0, LEN - TS * 128]], base=N, channel_multiplier=0) \
                        .then_inc(made.sem, 1)
                    pool.iota(ends[:, 2, :], pattern=[[0, LEN - TS * 128]], base=0, channel_multiplier=0) \
                        .then_inc(made.sem, 1)
                    pool.iota(fill[:, :], pattern=[[0, NCOL]], base=C, channel_multiplier=0).then_inc(made.sem, 1)
                    pool.iota(row_i[:, :], pattern=[[128, T]], base=0, channel_multiplier=1).then_inc(made.sem, 1)
                    pool.wait_ge(made.sem, 7)
                    pool.affine_select(out=ident[:, :], in_=ident[:, :], compare_op=ALU.not_equal, fill=1.0,
                                       base=0, pattern=[[-1, 128]], channel_multiplier=1)

                @block.vector
                def _(dve):
                    dve.wait_ge(loaded.sem, 16 * len(loads))
                    dve.tensor_scalar(cols[:, 7:8], cols[:, 6:7], 1.0, None, ALU.add)

        loaded.close(16 * len(loads)), made.close(7)

        def make_tables(tb, key, other, w):
            with ExitStack() as ph:
                rows_i = sb("rows_i", [TH, 3, 2, 128], i32, ph)
                rows_f = sb("rows_f", [TH, 4, 2, 128], fp32, ph)
                tmp = sb("tmp", [128, T], fp32, ph)
                firsts = sb("firsts", [1, T, 2], i32, ph)
                turned_at, made_at = setup_t.base, setup_c.base

                def windows(a, start):
                    return bass.AP(a.tensor, a.offset + start, [[EPT, TH], [EPT * TH, 2], [1, 128]])

                with nc.Block() as block:
                    @block.sync
                    def _(sp):
                        for dest, source in ((rows_i[:, 0], windows(key, 0)), (rows_i[:, 1], windows(key, 1)),
                                             (rows_i[:, 2], windows(other, 0)), (rows_f[:, 3], windows(w, 0))):
                            sp.dma_start(dest, source).then_inc(setup_dma.sem, 16)
                        first = bass.AP(key.tensor, key.offset + 1 + EPT, [[0, 1], [EPT, T - 1], [1, 2]])
                        sp.dma_start(firsts[:, 0:T - 1, :], first).then_inc(setup_dma.sem, 16)

                    @block.tensor
                    def _(pe):
                        pe.wait_ge(setup_c.sem, made_at + 1)
                        for a in range(4):
                            for half in range(2):
                                last = pe.transpose(bank[4 + a][:, half * TH:(half + 1) * TH], rows_f[:, a, half, :],
                                                    ident[0:TH, 0:TH])
                        last.then_inc(setup_t.sem, 1)

                    @block.vector
                    def _(dve):
                        dve.wait_ge(setup_dma.sem, setup_dma.base + 80)
                        dve.tensor_copy(rows_f[:, 0:3], rows_i[:, :]).then_inc(setup_c.sem, 1)
                        dve.wait_ge(setup_c.sem, setup_c.next())
                        dve.wait_ge(setup_t.sem, turned_at + 1)
                        dve.tensor_copy(tb.w[:, :], bank[7][:, 0:T])
                        dve.tensor_scalar(tb.other[:, :], bank[6][:, 0:T], 0.0, float(N - 1), ALU.max, ALU.min)
                        dve.tensor_copy(tb.key_p[:, :], bank[4][:, 0:T]).then_inc(setup_c.sem, 1)
                        dve.wait_ge(setup_c.sem, setup_c.next())
                        dve.tensor_scalar(tb.key_g[:, :], tb.key_p[:, :], 0.0, float(N - 1), ALU.max, ALU.min) \
                            .then_inc(setup_c.sem, 1)
                        dve.wait_ge(setup_c.sem, setup_c.next())
                        dve.tensor_tensor(tb.is_rep[:, :], tb.key_p[:, :], bank[5][:, 0:T], ALU.not_equal) \
                            .then_inc(setup_c.sem, 1)
                        dve.wait_ge(setup_c.sem, setup_c.next())
                        dve.tensor_scalar(tmp[:, :], tb.key_p[:, :], float(N), None, ALU.is_lt) \
                            .then_inc(setup_c.sem, 1)
                        dve.wait_ge(setup_c.sem, setup_c.next())
                        dve.tensor_tensor(tb.is_rep[:, :], tb.is_rep[:, :], tmp[:, :], ALU.mult) \
                            .then_inc(setup_c.sem, 1)
                        dve.wait_ge(setup_c.sem, setup_c.next())
                        dve.memset(tb.is_rep[0:1, :], 0.0).then_inc(setup_c.sem, 1)
                        dve.wait_ge(setup_c.sem, setup_c.next())
                        dve.tensor_copy(tb.rep_r[:, :], tb.is_rep[:, :]).then_inc(setup_c.sem, 1)
                        dve.wait_ge(setup_c.sem, setup_c.next())
                        dve.memset(tb.rep_r[0:1, :], 1.0).then_inc(setup_c.sem, 1)
                        dve.wait_ge(setup_c.sem, setup_c.next())
                        dve.tensor_scalar(tmp[:, :], tb.is_rep[:, :], -float(FAR), float(FAR), ALU.mult, ALU.add) \
                            .then_inc(setup_c.sem, 1)
                        dve.wait_ge(setup_c.sem, setup_c.next())
                        dve.tensor_tensor(tmp[:, :], tmp[:, :], tb.key_g[:, :], ALU.add).then_inc(setup_c.sem, 1)
                        dve.wait_ge(setup_c.sem, setup_c.next())
                        dve.tensor_copy(tb.key_s[:, :], tmp[:, :]).then_inc(setup_c.sem, 1)
                        dve.wait_ge(setup_c.sem, setup_c.next())
                        dve.tensor_copy(tb.key_r[:, :], tb.key_p[:, :]).then_inc(setup_c.sem, 1)
                        dve.wait_ge(setup_c.sem, setup_c.next())
                        dve.memset(tb.key_r[0:1, T - 1:T], float(N)).then_inc(setup_c.sem, 1)
                        dve.wait_ge(setup_c.sem, setup_c.next())
                        dve.tensor_copy(tb.key_r[0:1, 0:T - 1], firsts[:, 0:T - 1, 0]).then_inc(setup_c.sem, 1)
                        dve.wait_ge(setup_c.sem, setup_c.next())
                setup_dma.close(80), setup_t.close(1)

        make_tables(by_d, d["dst"], d["src"], d["edge_weight1"])

        idx_ready = sig("idx_ready")
        idx_ready2 = sig("idx_ready2")
        gathered = slots("gathered")
        fetched = slots("fetched")
        fetched2 = slots("fetched2")
        stored = slots("stored")
        stored2 = slots("stored2")
        scattered = slots("scattered")
        ln_made = sig("ln_made")
        ln2_made = sig("ln2_made")
        rooted = sig("rooted")
        rooted2 = sig("rooted2")
        h_made = sig("h_made")
        h2_made = sig("h2_made")
        turned = sig("turned")
        turned_sb = sig("turned_sb")
        turned2_sb = sig("turned2_sb")
        hid_ps = sig("hid_ps")
        hid_sb = sig("hid_sb")
        prod_ps = sig("prod_ps")
        prod_sb = sig("prod_sb")
        turned_b = sig("turned_b")
        turned_b_sb = sig("turned_b_sb")
        prod_b_ps = sig("prod_b_ps")
        prod_b_sb = sig("prod_b_sb")
        msg_made = sig("msg_made")
        same_made = sig("same_made")
        sum_ps = sig("sum_ps")
        carried = sig("carried")
        sum_sb = sig("sum_sb")
        exp_made = sig("exp_made")

        idx = sb("idx", [128, UNROLL, J], i32)
        idx2 = sb("idx2", [128, UNROLL, J], i32)

        def copy_index(dve, table, s, r, buf, ready, freed):
            freed()
            dve.tensor_copy(buf[:, r, :], table[:, bass.ds(J * s, J)]).then_inc(ready.sem, 1)

        def ln_stats(dve, made_, s, X, st, mv, P, n, first):
            for j in range(n):
                last = dve.bn_stats(st[0:P, j, :], X[0:P, j, :])
            last.then_inc(made_.sem, 1)
            dve.wait_ge(made_.sem, made_.at(s, first + 1))
            dve.sem_inc(dve_fence, 1)
            for j in range(n):
                last = dve.bn_aggr(mv[0:P, j, :], st[0:P, j, :])
            last.then_inc(made_.sem, 1)

        def ln_scale(dve, made_, rooted, s, mv, rs, nm, P, first, mask=None):
            dve.wait_ge(made_.sem, made_.at(s, first + 2))
            dve.wait_ge(rooted.sem, rooted.at(s))
            dve.reciprocal(rs[0:P, :], rs[0:P, :]).then_inc(made_.sem, 1)
            dve.wait_ge(made_.sem, made_.at(s, first + 3))
            if mask is not None:
                dve.tensor_tensor(rs[0:P, :], rs[0:P, :], mask, ALU.mult).then_inc(made_.sem, 1)
                dve.wait_ge(made_.sem, made_.at(s, first + 4))
            dve.scalar_tensor_tensor(out=nm[0:P, :], in0=mv[0:P, :, 0], scalar=-1.0, in1=rs[0:P, :],
                                     op0=ALU.mult, op1=ALU.mult).then_inc(made_.sem, 1)

        def layer_norm(dve, made_, rooted, s, X, st, mv, rs, nm, P, n, first, mask=None):
            ln_stats(dve, made_, s, X, st, mv, P, n, first)
            ln_scale(dve, made_, rooted, s, mv, rs, nm, P, first, mask)

        def root(act, made_, rooted, s, mv, rs, P, first):
            act.wait_ge(made_.sem, made_.at(s, first + 2))
            act.activation(rs[0:P, :], mv[0:P, :, 1], ACT.Sqrt, bias=ln_eps[0:P, :]).then_inc(rooted.sem, 1)

        def relu_norm(act, done, dest, X, rs, nm, P, n):
            for j in range(n):
                last = act.activation(dest[0:P, j, :], X[0:P, j, :], ACT.Relu, bias=nm[0:P, j:j + 1],
                                      scale=rs[0:P, j:j + 1])
            last.then_inc(done.sem, 1)

        x_in = slots("x_in")
        y_out = slots("y_out")
        x_out = slots("x_out")
        d_ln1 = sig("d_ln1").open(4)
        d_root, d_h, d_hT, d_hT_sb, d_prod = (sig(n).open(1) for n in ("d_root", "d_h", "d_hT", "d_hT_sb", "d_prod"))
        d_hid, d_hid_sb, d_x1 = (sig(n).open(2) for n in ("d_hid", "d_hid_sb", "d_x1"))
        e_ln = sig("e_ln").open(5)
        e_root, e_h, e_hT, e_hT_sb, e_yT, e_ystat, e_yT_sb, e_y, e_y_sb = (sig(n).open(1) for n in (
            "e_root", "e_h", "e_hT", "e_hT_sb", "e_yT", "e_ystat", "e_yT_sb", "e_y", "e_y_sb"))

        W = J * 128
        dense_mem = sb("dense_mem", [128, 4 * J4 * 2 * F])
        part = dense_mem.shape[1] // 8

        def shared(lo, hi, **sizes):
            dims = " ".join(sizes)
            return dense_mem[:, lo * part:hi * part].rearrange(f"p ({dims} f) -> p {dims} f", **sizes)

        dX = shared(0, 2, b=4, j=J)
        dOut = shared(2, 4, b=4, j=J)
        dh = shared(4, 5, b=2, j=J)
        dhT = shared(5, 6, b=2)
        dhid = shared(6, 8, b=2, m=2)
        dyT = shared(6, 7, b=2)
        dst6 = sb("dst6", [128, 2, J, 6])
        dmv = sb("dmv", [128, 2, J, 2])
        drs = sb("drs", [128, 2, J])
        dnm = sb("dnm", [128, 2, J])
        x_groups = by_group(d["x"], J)
        x2_groups = by_group(x2_d, J)
        y_groups = by_group(y_d, J)

        def rows_in(s):
            return TAIL if isinstance(s, int) and s == NF else 128

        def dense1_sp(sp):
            def emit(k, r):
                for s, b in steps_at(k, r, 0, ND):
                    P = rows_in(s)
                    if begun(s - 4):
                        sp.wait_ge(d_x1.sem, d_x1.at(s - 4))
                        sp.sem_inc(sp_fence, 1)
                    sp.dma_start(dX[0:P, b, :, :], group(x_groups, s, NF)).then_inc(x_in.sem(b), 16)
                for s, b in steps_at(k, r, 4, ND):
                    P = rows_in(s)
                    sp.wait_ge(d_x1.sem, d_x1.at(s))
                    sp.sem_inc(sp_fence, 1)
                    sp.dma_start(group(x2_groups, s, NF), dOut[0:P, b, :, :]).then_inc(x_out.sem(b), 16)
            return emit

        def dense1_dve(dve):
            def emit(k, r):
                for s, b in steps_at(k, r, 1, ND):
                    dve.wait_ge(x_in.sem(b), x_in.at(s, b))
                    if begun(s - 2):
                        dve.wait_ge(d_h.sem, d_h.at(s - 2))
                    ln_stats(dve, d_ln1, s, dX[:, b, :, :], dst6[:, b % 2], dmv[:, b % 2], rows_in(s), J, 0)
                for s, b in steps_at(k, r, 2, ND):
                    P = rows_in(s)
                    dve.wait_ge(d_hT.sem, d_hT.at(s))
                    if begun(s - 2):
                        dve.wait_ge(d_hid.sem, d_hid.at(s - 2))
                    dve.tensor_copy(dhT[:, b % 2, 0:J * P], bank[0][:, 0:J * P]).then_inc(d_hT_sb.sem, 1)
                for s, b in steps_at(k, r, 1, ND):
                    ln_scale(dve, d_ln1, d_root, s, dmv[:, b % 2], drs[:, b % 2], dnm[:, b % 2], rows_in(s), 0)
                for s, b in steps_at(k, r, 3, ND):
                    P = rows_in(s)
                    if begun(s - 4):
                        dve.wait_ge(x_out.sem(b), x_out.at(s - 4, b))
                    dve.tensor_tensor(dOut[0:P, b, :, :], dX[0:P, b, :, :],
                                      b2[0:P, :].unsqueeze(1).to_broadcast([P, J, F]), ALU.add).then_inc(d_x1.sem, 1)
                    dve.wait_ge(d_x1.sem, d_x1.at(s, 1))
                    dve.wait_ge(d_prod.sem, d_prod.at(s))
                    dve.tensor_tensor(dOut[0:P, b, :, :], dOut[0:P, b, :, :],
                                      bank[2][0:P, 0:W].rearrange("p (j f) -> p j f", j=J), ALU.add) \
                        .then_inc(d_x1.sem, 1)
            return emit

        def dense1_act(act):
            def emit(k, r):
                for s, b in steps_at(k, r, 1, ND):
                    root(act, d_ln1, d_root, s, dmv[:, b % 2], drs[:, b % 2], rows_in(s), 0)
                    act.wait_ge(d_ln1.sem, d_ln1.at(s))
                    if begun(s - 2):
                        act.wait_ge(d_hT.sem, d_hT.at(s - 2))
                    relu_norm(act, d_h, dh[:, b % 2], dX[:, b, :, :], drs[:, b % 2], dnm[:, b % 2], rows_in(s), J)
                for s, b in steps_at(k, r, 2, ND):
                    P = rows_in(s)
                    if begun(s - 2):
                        act.wait_ge(d_prod.sem, d_prod.at(s - 2))
                    act.wait_ge(d_hid.sem, d_hid.at(s))
                    for m in range(2):
                        act.activation(dhid[:, b % 2, m, 0:J * P], bank[1][:, m * W:m * W + J * P], ACT.Relu,
                                       bias=b1[:, m:m + 1]).then_inc(d_hid_sb.sem, 1)
            return emit

        def dense1_pe(pe):
            def emit(k, r):
                for s, b in steps_at(k, r, 2, ND):
                    P = rows_in(s)
                    pe.wait_ge(d_h.sem, d_h.at(s))
                    if begun(s - 1):
                        pe.wait_ge(d_hT_sb.sem, d_hT_sb.at(s - 1))
                    for j in range(J):
                        last = pe.transpose(bank[0][:, j * P:(j + 1) * P], dh[0:P, b % 2, j, :], ident[0:P, 0:P])
                    last.then_inc(d_hT.sem, 1)
                for s, b in steps_at(k, r, 3, ND):
                    P = rows_in(s)
                    pe.wait_ge(d_hid_sb.sem, d_hid_sb.at(s))
                    if begun(s - 1):
                        pe.wait_ge(d_x1.sem, d_x1.at(s - 1))
                    for j in range(J):
                        for m in range(2):
                            last = pe.matmul(bank[2][0:P, j * F:(j + 1) * F], dhid[:, b % 2, m, j * P:(j + 1) * P],
                                             w2lr[:, m, F:2 * F], start=(m == 0), stop=(m == 1))
                    last.then_inc(d_prod.sem, 1)
                for s, b in steps_at(k, r, 2, ND):
                    P = rows_in(s)
                    pe.wait_ge(d_hT_sb.sem, d_hT_sb.at(s))
                    if begun(s - 1):
                        pe.wait_ge(d_hid_sb.sem, d_hid_sb.at(s - 1))
                    for m in range(2):
                        pe.matmul(bank[1][:, m * W:m * W + J * P], w1r[:, m * 128:(m + 1) * 128],
                                  dhT[:, b % 2, 0:J * P], start=True, stop=True).then_inc(d_hid.sem, 1)
            return emit

        def dense2_sp(sp):
            def emit(k, r):
                for s, b in steps_at(k, r, 0, ND):
                    P = rows_in(s)
                    if begun(s - 4):
                        sp.wait_ge(e_h.sem, e_h.at(s - 4))
                        sp.sem_inc(sp_fence, 1)
                    sp.dma_start(dX[0:P, b, :, :], group(x2_groups, s, NF)).then_inc(x_in.sem(b), 16)
                for s, b in steps_at(k, r, 4, ND):
                    P = rows_in(s)
                    sp.wait_ge(e_y_sb.sem, e_y_sb.at(s))
                    sp.sem_inc(sp_fence, 1)
                    sp.dma_start(group(y_groups, s, NF), dOut[0:P, b, :, :]).then_inc(y_out.sem(b), 16)
            return emit

        def dense2_dve(dve):
            def emit(k, r):
                for s, b in steps_at(k, r, 1, ND):
                    dve.wait_ge(x_in.sem(b), x_in.at(s, b))
                    if begun(s - 2):
                        dve.wait_ge(e_h.sem, e_h.at(s - 2))
                    ln_stats(dve, e_ln, s, dX[:, b, :, :], dst6[:, b % 2], dmv[:, b % 2], rows_in(s), J, 0)
                for s, b in steps_at(k, r, 2, ND):
                    P = rows_in(s)
                    dve.wait_ge(e_hT.sem, e_hT.at(s))
                    if begun(s - 2):
                        dve.wait_ge(e_yT.sem, e_yT.at(s - 2))
                    dve.tensor_scalar(dhT[:, b % 2, 0:J * P], bank[0][:, 0:J * P], cols[:, 7:8], None,
                                      ALU.mult).then_inc(e_hT_sb.sem, 1)
                for s, b in steps_at(k, r, 1, ND):
                    ln_scale(dve, e_ln, e_root, s, dmv[:, b % 2], drs[:, b % 2], dnm[:, b % 2], rows_in(s), 0,
                             mask=no_out[0:rows_in(s), bass.ds(J * s, J)])
                for s, b in steps_at(k, r, 3, ND):
                    P = rows_in(s)
                    dve.wait_ge(e_yT_sb.sem, e_yT_sb.at(s))
                    dve.sem_inc(dve_fence, 1)
                    dve.bn_stats(ystat[:, bass.ds(s, 1), :].rearrange("p a c -> p (a c)"), dyT[:, b % 2, 0:J * P]) \
                        .then_inc(e_ystat.sem, 1)
                    dve.wait_ge(e_y.sem, e_y.at(s))
                    if begun(s - 4):
                        dve.wait_ge(y_out.sem(b), y_out.at(s - 4, b))
                    dve.tensor_copy(dOut[0:P, b, :, :], bank[2][0:P, 0:W].rearrange("p (j f) -> p j f", j=J)) \
                        .then_inc(e_y_sb.sem, 1)
            return emit

        def dense2_act(act):
            def emit(k, r):
                for s, b in steps_at(k, r, 1, ND):
                    root(act, e_ln, e_root, s, dmv[:, b % 2], drs[:, b % 2], rows_in(s), 0)
                    act.wait_ge(e_ln.sem, e_ln.at(s))
                    if begun(s - 2):
                        act.wait_ge(e_hT.sem, e_hT.at(s - 2))
                    relu_norm(act, e_h, dh[:, b % 2], dX[:, b, :, :], drs[:, b % 2], dnm[:, b % 2], rows_in(s), J)
                for s, b in steps_at(k, r, 2, ND):
                    P = rows_in(s)
                    act.wait_ge(e_yT.sem, e_yT.at(s))
                    if begun(s - 2):
                        act.wait_ge(e_y.sem, e_y.at(s - 2))
                    if begun(s - 2):
                        act.wait_ge(e_ystat.sem, e_ystat.at(s - 2))
                    act.activation(dyT[:, b % 2, 0:J * P], bank[1][:, 0:J * P], ACT.Copy).then_inc(e_yT_sb.sem, 1)
            return emit

        def dense2_pe(pe):
            def emit(k, r):
                for s, b in steps_at(k, r, 2, ND):
                    P = rows_in(s)
                    pe.wait_ge(e_h.sem, e_h.at(s))
                    if begun(s - 1):
                        pe.wait_ge(e_hT_sb.sem, e_hT_sb.at(s - 1))
                    for j in range(J):
                        last = pe.transpose(bank[0][:, j * P:(j + 1) * P], dh[0:P, b % 2, j, :], ident[0:P, 0:P])
                    last.then_inc(e_hT.sem, 1)
                for s, b in steps_at(k, r, 3, ND):
                    P = rows_in(s)
                    pe.wait_ge(e_yT_sb.sem, e_yT_sb.at(s))
                    if begun(s - 1):
                        pe.wait_ge(e_y_sb.sem, e_y_sb.at(s - 1))
                    for j in range(J):
                        last = pe.transpose(bank[2][0:P, j * F:(j + 1) * F], dyT[:, b % 2, j * P:(j + 1) * P],
                                            ident[:, :])
                    last.then_inc(e_y.sem, 1)
                for s, b in steps_at(k, r, 2, ND):
                    P = rows_in(s)
                    pe.wait_ge(e_hT_sb.sem, e_hT_sb.at(s))
                    if begun(s - 1):
                        pe.wait_ge(e_yT_sb.sem, e_yT_sb.at(s - 1))
                    pe.matmul(bank[1][:, 0:J * P], w1[:, :], dhT[:, b % 2, 0:J * P], start=True, stop=True) \
                        .then_inc(e_yT.sem, 1)
            return emit

        dense_passes = [
            {"sync": dense1_sp, "vector": dense1_dve, "scalar": dense1_act, "tensor": dense1_pe},
            {"sync": dense2_sp, "vector": dense2_dve, "scalar": dense2_act, "tensor": dense2_pe}]

        DLAG = 4
        dense_at = [0, 0]

        def run_phase(lag, programs, dense_iterations=0, steps=NS, cut=0, dense_pass=0, beside=None, beside_lag=0):
            n_dense = min(dense_iterations, max(0, ND + DLAG - dense_at[dense_pass]))
            if 0 < n_dense < ND + DLAG - dense_at[dense_pass]:
                n_dense = min(n_dense, steps + lag) // UNROLL * UNROLL
            total = max(steps + lag, n_dense, NS + beside_lag if beside else 0)
            off = dense_at[dense_pass]
            dense_of = dense_passes[dense_pass]

            def go(name, eng):
                streams = []
                if n_dense and name in dense_of:
                    lo = max(0, 2 * UNROLL - off)
                    streams.append((dense_of[name](eng), off, (0, n_dense), (lo, min(n_dense, NF - off))))
                if name in programs:
                    streams.append((programs[name](eng), 0, (0, steps + lag),
                                    (-(-(lag + UNROLL) // UNROLL) * UNROLL, steps - cut)))
                if beside and name in beside:
                    streams.append((beside[name](eng), 0, (0, NS + beside_lag),
                                    (-(-(beside_lag + UNROLL) // UNROLL) * UNROLL, NS)))
                if streams:
                    drive(eng, total, streams)
                for done in programs.get(name + "_end", []) + (beside or {}).get(name + "_end", []):
                    done(eng)

            with nc.Block() as block:
                block.sync(lambda sp: go("sync", sp))
                block.gpsimd(lambda pool: go("gpsimd", pool))
                block.scalar(lambda act: go("scalar", act))
                block.vector(lambda dve: go("vector", dve))
                block.tensor(lambda pe: go("tensor", pe))
            dense_at[dense_pass] += n_dense

        def all_stored(signal, steps=NS):
            def wait(eng):
                for b in range(len(signal.sems)):
                    if steps > b:
                        eng.wait_ge(signal.sem(b), signal.at(steps - 1 - (steps - 1 - b) % len(signal.sems), b))
            return wait

        ST, SA, SB, SS = bank[4], bank[5], bank[6], bank[7]
        SB4 = SB[:, :].rearrange("p (j c) -> p j c", j=J)
        SS4 = SS[:, :].rearrange("p (j c) -> p j c", j=J)

        def jview(ap):
            return ap.rearrange("p (j f) -> p j f", j=J)

        def gather(pool, table, s, b, buf):
            for j in range(J):
                pool.indirect_dma_start(buf[:, b, j, :], None, table,
                                        bass.IndirectOffsetOnAxis(ap=idx[:, b, j:j + 1], axis=0)) \
                    .then_inc(gathered.sem(b), 16)

        tables = [by_d]

        def build_same(dve, s, b):
            if begun(s - 2):
                dve.wait_ge(sum_ps.sem, sum_ps.at(s - 2))
            dve.tensor_tensor(S[:, b % 2, :, :], key_q[:, bass.ds(J * s, J), :],
                              tables[0].key_p[:, bass.ds(J * s, J)].unsqueeze(2).to_broadcast([128, J, 128]),
                              ALU.is_equal).then_inc(same_made.sem, 1)

        def sum_segments(pe, s, b, width):
            pe.wait_ge(same_made.sem, same_made.at(s))
            pe.wait_ge(msg_made.sem, msg_made.at(s))
            if begun(s - 1):
                pe.wait_ge(sum_sb.sem, sum_sb.at(s - 1))
            for j in range(J):
                if not (isinstance(s, int) and J * s + j == 0):
                    pe.wait_ge(carried.sem, carried.at(s, j))
                pe.matmul(SS4[:, j, 0:width], S[:, b % 2, j, :], M[:, b % 2, j, 0:width], start=True, stop=True) \
                    .then_inc(sum_ps.sem, 1)

        def carry(act, s, b, width, tiles=range(J)):
            for j in tiles:
                if isinstance(s, int) and J * s + j == T - 1:
                    continue
                act.wait_ge(sum_ps.sem, sum_ps.at(s, j + 1))
                nb, nj = (b % 2, j + 1) if j + 1 < J else ((b + 1) % 2, 0)
                if nj == 0:
                    act.wait_ge(msg_made.sem, msg_made.at(s + 1))
                act.activation(M[0:1, nb, nj, 0:width], SS4[0:1, j, 0:width], ACT.Copy).then_inc(carried.sem, 1)

        def sums_ready(dve, s):
            dve.wait_ge(sum_ps.sem, sum_ps.at(s))
            dve.wait_ge(carried.sem, carried.at(s, J - 1 if isinstance(s, int) and s == NS - 1 else J))

        def close_sums():
            same_made.close(NS), sum_ps.close(J * NS), carried.close(T - 1)

        mark_rows_b = sb("mark_rows_b", [128, UNROLL, J], i32)
        mark_idx = sb("mark_idx", [128, UNROLL, J], i32)
        found = sb("found", [128, UNROLL, J], i32)
        mark_ready = sig("mark_ready")
        marked = slots("marked")
        found_sb = sig("found_sb").open(1)

        def mark_rows(tb, table):
            def mark_dve(dve):
                def emit(k, r):
                    for s, b in steps_at(k, r, 0, NS):
                        if begun(s - 4):
                            dve.wait_ge(marked.sem(b), marked.at(s - 4, b))
                        dve.sem_inc(dve_fence, 1)
                        dve.tensor_copy(mark_idx[:, b, :], tb.key_s[:, bass.ds(J * s, J)]).then_inc(mark_ready.sem, 1)
                        dve.tensor_copy(mark_rows_b[:, b, :], row_i[:, bass.ds(J * s, J)]).then_inc(mark_ready.sem, 1)
                return emit

            def mark_pool(pool):
                def emit(k, r):
                    for s, b in steps_at(k, r, 0, NS):
                        pool.wait_ge(mark_ready.sem, mark_ready.at(s))
                        pool.sem_inc(pool_fence, 1)
                        for j in range(J):
                            pool.indirect_dma_start(
                                table, bass.IndirectOffsetOnAxis(ap=mark_idx[:, b, j:j + 1], axis=0),
                                mark_rows_b[:, b, j:j + 1], None, bounds_check=N - 1, oob_is_err=False) \
                                .then_inc(marked.sem(b), 16)
                return emit

            mark_ready.open(2), marked.open(J)
            return {"vector": mark_dve, "gpsimd": mark_pool, "gpsimd_end": [all_stored(marked)]}

        def find_rows():
            def find_dve(dve):
                def emit(k, r):
                    for s, b in steps_at(k, r, 0, NS):
                        if begun(s - 4):
                            dve.wait_ge(marked.sem(b), marked.at(s - 4, b))
                        dve.sem_inc(dve_fence, 1)
                        dve.tensor_copy(mark_idx[:, b, :], by_d.other[:, bass.ds(J * s, J)]).then_inc(mark_ready.sem, 1)
                    for s, b in steps_at(k, r, 2, NS):
                        dve.wait_ge(marked.sem(b), marked.at(s, b))
                        dve.sem_inc(dve_fence, 1)
                        dve.tensor_copy(ss_i[:, bass.ds(J * s, J)], found[:, b, :]).then_inc(found_sb.sem, 1)
                return emit

            def find_pool(pool):
                def emit(k, r):
                    for s, b in steps_at(k, r, 0, NS):
                        pool.wait_ge(mark_ready.sem, mark_ready.at(s))
                        pool.sem_inc(pool_fence, 1)
                        if begun(s - 4):
                            pool.wait_ge(found_sb.sem, found_sb.at(s - 4))
                            pool.sem_inc(pool_fence, 1)
                        for j in range(J):
                            pool.indirect_dma_start(
                                found[:, b, j:j + 1], None, rep_of,
                                bass.IndirectOffsetOnAxis(ap=mark_idx[:, b, j:j + 1], axis=0)) \
                                .then_inc(marked.sem(b), 16)
                return emit

            mark_ready.open(1), marked.open(J)
            return {"vector": find_dve, "gpsimd": find_pool}

        hist_made = sig("hist_made").open(1)
        hist_used = sig("hist_used").open(1)
        place_read = sig("place_read").open(1)
        place_next = sig("place_next").open(1)
        place_out = sig("place_out").open(2)
        sort_c = sig("sort_c")
        sort_p = sig("sort_p")
        fp16 = mybir.dt.float16
        B = DIGITS[0][1]

        def sort_pass(fields, shift, bins, out_rows, beside=None):
            at_c, at_p = sort_c.base, sort_p.base
            with ExitStack() as ph:
                pay = sb("pay", [128, TS, 4], i32, ph)
                col = sb("col", [128, 3, TS], i32, ph)
                dig_i = sb("dig_i", [128, TS], i32, ph)
                dig = sb("dig", [128, TS], fp32, ph)
                bin_no = sb("bin_no", [128, B], fp16, ph)
                bin_f = sb("bin_f", [128, B], fp32, ph)
                hot = sb("hot", [128, 4, B], fp16, ph)
                own = sb("own", [128, B], fp16, ph)
                below = sb("below", [128, 2, B + 1], fp32, ph)
                picked = sb("picked", [128, 2, B], fp32, ph)
                place = sb("place", [128, 4, 1], fp32, ph)
                place_i = sb("place_i", [128, 4, 1], i32, ph)
                row = sb("row", [128, 4, 4], i32, ph)
                lower_f = sb("lower_f", [128, 128], fp32, ph)
                lower = sb("lower", [128, 128], fp16, ph)
                ones = sb("ones", [128, 128], fp16, ph)
                ident16 = sb("ident16", [128, 128], fp16, ph)
                n_in = 1 if not isinstance(fields, list) else 3
                with nc.Block() as block:
                    @block.sync
                    def _(sp):
                        if n_in == 1:
                            sp.dma_start(pay[:, :, :], fields.rearrange("(p t) c -> p t c", t=TS)) \
                                .then_inc(setup_dma.sem, 16)
                        else:
                            for i, a in enumerate(fields):
                                sp.dma_start(col[:, i, :], a[1:1 + 128 * TS].rearrange("(p t) -> p t", t=TS)) \
                                    .then_inc(setup_dma.sem, 16)

                    @block.gpsimd
                    def _(pool):
                        pool.iota(bin_f[:, :], pattern=[[1, B]], base=0, channel_multiplier=0,
                                  allow_small_or_imprecise_dtypes=True).then_inc(made.sem, 1)
                        pool.memset(lower_f[:, :], 1.0).then_inc(made.sem, 1)
                        pool.wait_ge(made.sem, made.base + 2)
                        pool.affine_select(out=lower_f[:, :], in_=lower_f[:, :], compare_op=ALU.is_gt, fill=0.0,
                                           base=0, pattern=[[1, 128]], channel_multiplier=-1).then_inc(made.sem, 1)

                    @block.vector
                    def _(dve):
                        dve.wait_ge(setup_dma.sem, setup_dma.base + 16 * n_in)
                        if n_in == 3:
                            dve.memset(pay[:, :, 3:4], 0).then_inc(sort_c.sem, 1)
                            dve.wait_ge(sort_c.sem, sort_c.next())
                            for i in range(2):
                                dve.tensor_copy(pay[:, :, i], col[:, i, :]).then_inc(sort_c.sem, 1)
                                dve.wait_ge(sort_c.sem, sort_c.next())
                            dve.tensor_copy(pay[:, :, 2:3].bitcast(fp32),
                                            col[:, 2, :].bitcast(fp32).unsqueeze(2)).then_inc(sort_c.sem, 1)
                            dve.wait_ge(sort_c.sem, sort_c.next())
                        dve.tensor_scalar(dig_i[:, :], pay[:, :, 0], shift, bins - 1,
                                          ALU.logical_shift_right, ALU.bitwise_and).then_inc(sort_c.sem, 1)
                        dve.wait_ge(sort_c.sem, sort_c.next())
                        dve.wait_ge(made.sem, made.base + 3)
                        dve.tensor_copy(dig[:, :], dig_i[:, :])
                        dve.tensor_copy(bin_no[:, :], bin_f[:, :])
                        dve.tensor_copy(lower[:, :], lower_f[:, :])
                        dve.tensor_copy(ident16[:, :], ident[:, :])
                        dve.memset(ones[:, :], 1.0).then_inc(sort_c.sem, 1)
                        dve.wait_ge(sort_c.sem, sort_c.next())

                        def emit(k, r):
                            for t, b in steps_at(k, r, 0, TS):
                                if begun(t - 4):
                                    dve.wait_ge(hist_used.sem, hist_used.at(t - 4))
                                dve.tensor_scalar(hot[:, b, :], bin_no[:, :], dig[:, bass.ds(t, 1)], None,
                                                  ALU.is_equal).then_inc(hist_made.sem, 1)
                        drive(dve, TS, [(emit, 0, (0, TS), (UNROLL, TS))])
                        dve.wait_ge(hist_used.sem, hist_used.at(TS - 1))
                        dve.tensor_copy(own[:, :], bank[4][:, :]).then_inc(sort_c.sem, 1)
                        dve.wait_ge(sort_c.sem, sort_c.next())
                        dve.wait_ge(sort_p.sem, at_p + 1)
                        dve.memset(below[:, :, 0:1], 0.0).then_inc(sort_c.sem, 1)
                        dve.wait_ge(sort_c.sem, sort_c.next())
                        dve.tensor_copy(below[:, 0, 1:B + 1], bank[5][:, :]).then_inc(sort_c.sem, 1)
                        dve.wait_ge(sort_c.sem, sort_c.next())
                        n, cur = 1, 0
                        while n < B:
                            dve.tensor_copy(below[:, 1 - cur, 1:n + 1], below[:, cur, 1:n + 1]) \
                                .then_inc(sort_c.sem, 1)
                            dve.wait_ge(sort_c.sem, sort_c.next())
                            dve.tensor_tensor(below[:, 1 - cur, n + 1:B + 1], below[:, cur, n + 1:B + 1],
                                              below[:, cur, 1:B + 1 - n], ALU.add).then_inc(sort_c.sem, 1)
                            dve.wait_ge(sort_c.sem, sort_c.next())
                            n, cur = 2 * n, 1 - cur
                        dve.tensor_copy(picked[:, 0, :], below[:, cur, 0:B]).then_inc(sort_c.sem, 1)
                        dve.wait_ge(sort_c.sem, sort_c.next())

                    @block.tensor
                    def _(pe):
                        pe.wait_ge(sort_c.sem, at_c + (4 if n_in == 3 else 0) + 2)

                        def emit(k, r):
                            for t, b in steps_at(k, r, 0, TS):
                                pe.wait_ge(hist_made.sem, hist_made.at(t))
                                first, last = isinstance(t, int) and t == 0, isinstance(t, int) and t == TS - 1
                                pe.matmul(bank[4][:, :], ident16[:, :], hot[:, b, :], start=first, stop=last,
                                          skip_group_check=True).then_inc(hist_used.sem, 1)
                        drive(pe, TS, [(emit, 0, (0, TS), (UNROLL, (TS - 1) // UNROLL * UNROLL))])
                        pe.wait_ge(sort_c.sem, at_c + (4 if n_in == 3 else 0) + 3)
                        pe.matmul(bank[5][:, :], ones[:, :], own[:, :], start=True, stop=True).then_inc(sort_p.sem, 1)
                hist_made.close(TS), hist_used.close(TS), setup_dma.close(16 * n_in), made.close(3), sort_p.close(1)

                idx_ready.open(1)
                hist_used.open(1)
                at_p = sort_p.base

                def sort_dve(dve):
                    dve.wait_ge(sort_p.sem, at_p + 1)

                    def emit(k, r):
                        for t, b in steps_at(k, r, 0, TS):
                            if begun(t - 4):
                                dve.wait_ge(place_next.sem, place_next.at(t - 4))
                            dve.tensor_scalar(hot[:, b, :], bin_no[:, :], dig[:, bass.ds(t, 1)], None,
                                              ALU.is_equal).then_inc(hist_made.sem, 1)
                        for t, b in steps_at(k, r, 1, TS):
                            dve.wait_ge(hist_made.sem, hist_made.at(t))
                            if isinstance(t, int) and t < 2:
                                dve.wait_ge(sort_p.sem, at_p + 2)
                            if begun(t - 2):
                                dve.wait_ge(place_next.sem, place_next.at(t - 2))
                            if begun(t - 4):
                                dve.wait_ge(scattered.sem(b), scattered.at(t - 4, b))
                            dve.tensor_tensor_reduce(out=picked[:, b % 2, :], in0=hot[:, b, :],
                                                     in1=bank[4 + b % 2][:, :], scale=1.0, scalar=0.0, op0=ALU.mult,
                                                     op1=ALU.add, accum_out=place[:, b, :]).then_inc(place_read.sem, 1)
                            dve.tensor_copy(row[:, b, 0:2], pay[:, bass.ds(t, 1), 0:2].rearrange("p a c -> p (a c)"))
                            dve.tensor_copy(row[:, b, 2:4].bitcast(fp32),
                                            pay[:, bass.ds(t, 1), 2:4].bitcast(fp32).rearrange("p a c -> p (a c)")) \
                                .then_inc(place_out.sem, 1)
                            dve.wait_ge(place_read.sem, place_read.at(t))
                            dve.tensor_copy(place_i[:, b, :], place[:, b, :]).then_inc(place_out.sem, 1)
                    return emit

                def sort_pe(pe):
                    for i in range(2):
                        pe.matmul(bank[4 + i][:, :], ident[:, :], picked[:, 0, :], start=True, stop=False,
                                  skip_group_check=True)
                        last = pe.matmul(bank[4 + i][:, :], lower[:, :], own[:, :], start=False, stop=False,
                                         skip_group_check=True)
                    last.then_inc(sort_p.sem, 1)

                    def emit(k, r):
                        if isinstance(k, int) and k == 0:
                            pe.wait_ge(hist_made.sem, hist_made.at(0))
                            pe.matmul(bank[5][:, :], ident16[:, :], hot[:, 0, :], start=False, stop=True,
                                      skip_group_check=True).then_inc(sort_p.sem, 1)
                        for t, b in steps_at(k, r, 1, TS):
                            pe.wait_ge(place_read.sem, place_read.at(t))
                            if not (isinstance(t, int) and t >= TS - 2):
                                pe.wait_ge(hist_made.sem, hist_made.at(t + 1))
                                for u in (b, (b + 1) % 4):
                                    last = pe.matmul(bank[4 + b % 2][:, :], ident16[:, :], hot[:, u, :], start=False,
                                                     stop=True, skip_group_check=True)
                                last.then_inc(place_next.sem, 1)
                    return emit

                def sort_pool(pool):
                    def emit(k, r):
                        for t, b in steps_at(k, r, 1, TS):
                            pool.wait_ge(place_out.sem, place_out.at(t))
                            pool.sem_inc(pool_fence, 1)
                            pool.indirect_dma_start(
                                out_rows, bass.IndirectOffsetOnAxis(ap=place_i[:, b, :], axis=0), row[:, b, :], None) \
                                .then_inc(scattered.sem(b), 16)
                    return emit

                scattered.open(1)
                run_phase(1, {"vector": sort_dve, "tensor": sort_pe, "gpsimd": sort_pool,
                              "gpsimd_end": [all_stored(scattered, TS)]}, DENSE_IN_SORT, TS, cut=2,
                          beside=beside)
                hist_made.close(TS), place_read.close(TS), place_next.close(TS - 2), place_out.close(2 * TS)
                scattered.close(TS), sort_p.close(2)

        DENSE_IN_SORT = TS // UNROLL * UNROLL
        sort_pass([d["src"], d["dst"], d["edge_weight"].bitcast(i32)], *DIGITS[0], sorted_d[0])
        sort_pass(sorted_d[0], *DIGITS[1], sorted_d[1], beside=mark_rows(by_d, rep_of))
        mark_ready.close(2 * NS), marked.close(NS)

        with ExitStack() as ph:
            pay = sb("pay", [128, TS, 4], i32, ph)
            col = sb("col", [128, 3, TS], i32, ph)
            at_c = sort_c.base
            with nc.Block() as block:
                @block.sync
                def _(sp):
                    sp.dma_start(pay[:, :, :], sorted_d[1].rearrange("(p t) c -> p t c", t=TS)).then_inc(setup_dma.sem, 16)
                    sp.wait_ge(sort_c.sem, at_c + 3)
                    for i, a in enumerate((by_src["key"], by_src["other"], by_src["w"].bitcast(i32))):
                        sp.dma_start(a[1:1 + 128 * TS].rearrange("(p t) -> p t", t=TS), col[:, i, :]) \
                            .then_inc(setup_dma.sem, 16)
                    sp.wait_ge(setup_dma.sem, setup_dma.base + 64)

                @block.vector
                def _(dve):
                    dve.wait_ge(setup_dma.sem, setup_dma.base + 16)
                    for i in range(2):
                        dve.tensor_copy(col[:, i, :], pay[:, :, i]).then_inc(sort_c.sem, 1)
                        dve.wait_ge(sort_c.sem, sort_c.next())
                    dve.tensor_copy(col[:, 2, :].bitcast(fp32).unsqueeze(2), pay[:, :, 2:3].bitcast(fp32)) \
                        .then_inc(sort_c.sem, 1)
                    dve.wait_ge(sort_c.sem, sort_c.next())
            setup_dma.close(64)
        make_tables(by_s, by_src["key"], by_src["other"], by_src["w"])

        key_q = sb("key_q", [128, T, 128])
        QC = 6 if T % 6 == 0 else 2
        TC = T // QC

        def load_key_q(sp, key):
            dst_b = bass.AP(key.tensor, key.offset + 1, [[0, 128], [EPT, T], [1, EPT]])
            for c in range(QC):
                sp.dma_start(key_q[:, c * TC:(c + 1) * TC, 1:128].bitcast(i32), dst_b[:, c * TC:(c + 1) * TC, :]) \
                    .then_inc(loaded.sem, 16)

        def make_key_q(dve):
            dve.wait_ge(loaded.sem, loaded.base + 16 * QC)
            for t0 in range(0, T, TC):
                last = dve.tensor_copy(key_q[:, t0:t0 + TC, 1:128], key_q[:, t0:t0 + TC, 1:128].bitcast(i32))
            last.then_inc(setup_c.sem, 1)
            dve.wait_ge(setup_c.sem, setup_c.next())
            dve.tensor_copy(key_q[:, :, 0:1], key_q[:, :, 127:128]).then_inc(setup_c.sem, 1)
            dve.wait_ge(setup_c.sem, setup_c.next())

        def reload_key_q(key):
            with nc.Block() as block:
                block.sync(lambda sp: load_key_q(sp, key))
                block.vector(lambda dve: make_key_q(dve))
            loaded.close(16 * QC)

        reload_key_q(d["dst"])
        G = sb("G", [128, 4, J, F], fp32)
        L = sb("L", [128, 4, 3, J, F], fp32)
        XE = sb("XE", [128, 4, J, 2 * F], fp32)
        OUT = sb("OUT", [128, 4, J, F], fp32)
        M = sb("M", [128, 2, J, ACC_W], fp32)
        S = sb("S", [128, 2, J, 128], fp32)
        h = sb("h", [128, 2, J, F], fp32)
        hb = sb("hb", [128, 2, J, F], fp32)
        hT = sb("hT", [128, 2, W], fp32)
        pair = sb("pair", [128, 2, 2, W])
        aT, hbT = pair[:, 0], pair[:, 1]
        hid = sb("hid", [128, 2, 2, W], fp32)
        haT = sb("haT", [128, 2, 2 * W], fp32)
        est = [sb(f"est{i}", [128, 2, J, 6], fp32) for i in range(2)]
        emv = [sb(f"emv{i}", [128, 2, J, 2], fp32) for i in range(2)]
        ers = [sb(f"ers{i}", [128, 2, J], fp32) for i in range(2)]
        enm = [sb(f"enm{i}", [128, 2, J], fp32) for i in range(2)]
        nrm = sb("nrm", [128, 2, J, HEADS], fp32)
        sc = sb("sc", [128, 2, J, HEADS], fp32)

        LAG = 5
        idx_ready.open(1), gathered.open(J), stored.open(1), stored2.open(1)
        ln_made.open(4), rooted.open(1), msg_made.open(1), same_made.open(1), sum_ps.open(J), carried.open(J), sum_sb.open(3)
        xs_v, a0_v = by_step(xs_d), by_step(a0_d)

        def l0a_dve(dve):
            dve.memset(M[:, :, :, F:F + 1], 1.0)

            def emit(k, r):
                for s, b in steps_at(k, r, 0, NS):
                    if begun(s - UNROLL):
                        dve.wait_ge(gathered.sem(b), gathered.at(s - UNROLL, b))
                    dve.sem_inc(dve_fence, 1)
                    dve.tensor_copy(idx[:, b, :], by_d.other[:, bass.ds(J * s, J)]).then_inc(idx_ready.sem, 1)
                for s, b in steps_at(k, r, 5, NS):
                    sums_ready(dve, s)
                    if begun(s - 4):
                        dve.wait_ge(stored2.sem(b), stored2.at(s - 4, b))
                    dve.tensor_scalar(nrm[:, b % 2, :, 0:1], SS4[:, :, F:F + 1], 1.0, None, ALU.max) \
                        .then_inc(sum_sb.sem, 1)
                    dve.wait_ge(sum_sb.sem, sum_sb.at(s, 1))
                    dve.sem_inc(dve_fence, 1)
                    dve.reciprocal(rcnt[:, bass.ds(J * s, J)], nrm[:, b % 2, :, 0]).then_inc(sum_sb.sem, 1)
                    dve.wait_ge(sum_sb.sem, sum_sb.at(s, 2))
                    dve.tensor_tensor(OUT[:, b], SS4[:, :, 0:F],
                                      rcnt[:, bass.ds(J * s, J)].unsqueeze(2).to_broadcast([128, J, F]), ALU.mult) \
                        .then_inc(sum_sb.sem, 1)
                for s, b in steps_at(k, r, 3, NS):
                    build_same(dve, s, b)
                for s, b in steps_at(k, r, 2, NS):
                    dve.wait_ge(gathered.sem(b), gathered.at(s, b))
                    if begun(s - 2):
                        dve.wait_ge(msg_made.sem, msg_made.at(s - 2))
                    layer_norm(dve, ln_made, rooted, s, G[:, b], est[0][:, b % 2], emv[0][:, b % 2], ers[0][:, b % 2],
                               enm[0][:, b % 2], 128, J, 0)
            return emit

        def l0a_pool(pool):
            def emit(k, r):
                for s, b in steps_at(k, r, 1, NS):
                    pool.wait_ge(idx_ready.sem, idx_ready.at(s))
                    pool.sem_inc(pool_fence, 1)
                    if begun(s - 4):
                        pool.wait_ge(msg_made.sem, msg_made.at(s - 4))
                        pool.sem_inc(pool_fence, 1)
                    if begun(s - 4):
                        pool.wait_ge(stored.sem(b), stored.at(s - 4, b))
                        pool.sem_inc(pool_fence, 1)
                    gather(pool, d["x"], s, b, G)
            return emit

        def l0a_sp(sp):
            def emit(k, r):
                for s, b in steps_at(k, r, 2, NS):
                    sp.wait_ge(gathered.sem(b), gathered.at(s, b))
                    sp.sem_inc(sp_fence, 1)
                    sp.dma_start(xs_v[s], G[:, b]).then_inc(stored.sem(b), 16)
                for s, b in steps_at(k, r, 5, NS):
                    sp.wait_ge(sum_sb.sem, sum_sb.at(s))
                    sp.sem_inc(sp_fence, 1)
                    sp.dma_start(a0_v[s], OUT[:, b]).then_inc(stored2.sem(b), 16)
            return emit

        def l0a_act(act):
            def emit(k, r):
                for s, b in steps_at(k, r, 4, NS):
                    carry(act, s, b, F + 1)
                for s, b in steps_at(k, r, 2, NS):
                    root(act, ln_made, rooted, s, emv[0][:, b % 2], ers[0][:, b % 2], 128, 0)
                    act.wait_ge(ln_made.sem, ln_made.at(s))
                    if begun(s - 2):
                        act.wait_ge(sum_ps.sem, sum_ps.at(s - 2))
                    relu_norm(act, msg_made, M[:, b % 2, :, 0:F], G[:, b], ers[0][:, b % 2], enm[0][:, b % 2], 128, J)
            return emit

        def l0a_pe(pe):
            def emit(k, r):
                for s, b in steps_at(k, r, 4, NS):
                    sum_segments(pe, s, b, F + 1)
            return emit

        run_phase(LAG, {"vector": l0a_dve, "gpsimd": l0a_pool, "sync": l0a_sp, "scalar": l0a_act, "tensor": l0a_pe,
                        "sync_end": [all_stored(stored), all_stored(stored2)]}, 104,
                  beside=find_rows(), beside_lag=2)
        mark_ready.close(NS), marked.close(NS), found_sb.close(NS)
        idx_ready.close(NS), gathered.close(NS), stored.close(NS), stored2.close(NS)
        ln_made.close(4 * NS), rooted.close(NS), msg_made.close(NS), sum_sb.close(3 * NS)
        close_sums()

        LAG = 7
        fetched.open(1), h_made.open(1), turned.open(1), turned_sb.open(1)
        hid_ps.open(2), hid_sb.open(2), prod_ps.open(1), prod_sb.open(2), sum_sb.open(1), gathered.open(J)
        x1s_v, a1_v = by_step(x1s_d), by_step(a1_d)

        def hidden_pe(pe, s, b):
            pe.wait_ge(turned_sb.sem, turned_sb.at(s))
            if begun(s - 1):
                pe.wait_ge(hid_sb.sem, hid_sb.at(s - 1))
            for m in range(2):
                pe.matmul(SA[:, m * W:(m + 1) * W], w1l[:, m * 128:(m + 1) * 128], haT[:, b % 2, W:2 * W],
                          start=True, stop=False)
                pe.matmul(SA[:, m * W:(m + 1) * W], w1r[:, m * 128:(m + 1) * 128], haT[:, b % 2, 0:W],
                          start=False, stop=True).then_inc(hid_ps.sem, 1)

        def product_pe(pe, s, b, both):
            pe.wait_ge(hid_sb.sem, hid_sb.at(s))
            if begun(s - 1):
                pe.wait_ge(prod_sb.sem, prod_sb.at(s - 1))
            for j in range(J):
                dest = SB4[:, j, :] if both else SB[:, j * F:(j + 1) * F]
                for m in range(2):
                    last = pe.matmul(dest, hid[:, b % 2, m, j * 128:(j + 1) * 128],
                                     w2lr[:, m, 0:2 * F] if both else w2lr[:, m, F:2 * F],
                                     start=(m == 0), stop=(m == 1))
            last.then_inc(prod_ps.sem, 1)

        L0 = L[:, :, 0, :, :]

        def turn_pe(pe, s, b, aggregated):
            pe.wait_ge(h_made.sem, h_made.at(s))
            if begun(s - 1):
                pe.wait_ge(turned_sb.sem, turned_sb.at(s - 1))
            for i, rows_ in enumerate((h[:, b % 2], aggregated[:, b])):
                for j in range(J):
                    last = pe.transpose(ST[:, i * W + j * 128:i * W + (j + 1) * 128], rows_[:, j, :], ident[:, :])
            last.then_inc(turned.sem, 1)

        def turned_dve(dve, s, b):
            dve.wait_ge(turned.sem, turned.at(s))
            if begun(s - 2):
                dve.wait_ge(hid_ps.sem, hid_ps.at(s - 2))
            dve.tensor_copy(haT[:, b % 2, :], ST[:, :]).then_inc(turned_sb.sem, 1)

        def hidden_act(act, s, b):
            if begun(s - 2):
                act.wait_ge(prod_ps.sem, prod_ps.at(s - 2))
            act.wait_ge(hid_ps.sem, hid_ps.at(s))
            for m in range(2):
                act.activation(hid[:, b % 2, m, :], SA[:, m * W:(m + 1) * W], ACT.Relu, bias=b1[:, m:m + 1]) \
                    .then_inc(hid_sb.sem, 1)

        def l0b_dve(dve):
            def emit(k, r):
                for s, b in steps_at(k, r, 7, NS):
                    sums_ready(dve, s)
                    if begun(s - 4):
                        dve.wait_ge(stored2.sem(b), stored2.at(s - 4, b))
                    dve.tensor_tensor(OUT[:, b], SS4[:, :, 0:F],
                                      rcnt[:, bass.ds(J * s, J)].unsqueeze(2).to_broadcast([128, J, F]), ALU.mult) \
                        .then_inc(sum_sb.sem, 1)
                for s, b in steps_at(k, r, 0, NS):
                    if begun(s - UNROLL):
                        dve.wait_ge(gathered.sem(b), gathered.at(s - UNROLL, b))
                    dve.sem_inc(dve_fence, 1)
                    dve.tensor_copy(idx[:, b, :], ss_i[:, bass.ds(J * s, J)]).then_inc(idx_ready.sem, 1)
                for s, b in steps_at(k, r, 5, NS):
                    build_same(dve, s, b)
                for s, b in steps_at(k, r, 5, NS):
                    dve.wait_ge(prod_ps.sem, prod_ps.at(s))
                    if begun(s - 2):
                        dve.wait_ge(sum_ps.sem, sum_ps.at(s - 2))
                    if begun(s - 2):
                        dve.wait_ge(carried.sem, carried.at(s - 2))
                    dve.tensor_copy(M[:, b % 2, :, 0:F], SB4[:, :, 0:F]).then_inc(msg_made.sem, 1)
                    if begun(s - 4):
                        dve.wait_ge(stored.sem(b), stored.at(s - 4, b))
                    dve.tensor_tensor(XE[:, b, :, 0:F], L0[:, b], SB4[:, :, F:2 * F], ALU.add) \
                        .then_inc(prod_sb.sem, 1)
                    dve.wait_ge(prod_sb.sem, prod_sb.at(s, 1))
                    dve.tensor_tensor(XE[:, b, :, 0:F], XE[:, b, :, 0:F],
                                      b2[:, :].unsqueeze(1).to_broadcast([128, J, F]), ALU.add) \
                        .then_inc(prod_sb.sem, 1)
                for s, b in steps_at(k, r, 3, NS):
                    turned_dve(dve, s, b)
                for s, b in steps_at(k, r, 2, NS):
                    dve.wait_ge(fetched.sem(b), fetched.at(s, b))
                    if begun(s - 2):
                        dve.wait_ge(h_made.sem, h_made.at(s - 2))
                    ln_stats(dve, ln_made, s, L0[:, b], est[0][:, b % 2], emv[0][:, b % 2], 128, J, 0)
                for s, b in steps_at(k, r, 2, NS):
                    ln_scale(dve, ln_made, rooted, s, emv[0][:, b % 2], ers[0][:, b % 2], enm[0][:, b % 2], 128, 0)
            return emit

        def l0b_pool(pool):
            def emit(k, r):
                for s, b in steps_at(k, r, 1, NS):
                    pool.wait_ge(idx_ready.sem, idx_ready.at(s))
                    pool.sem_inc(pool_fence, 1)
                    if begun(s - 4):
                        pool.wait_ge(turned.sem, turned.at(s - 4))
                        pool.sem_inc(pool_fence, 1)
                    gather(pool, a0_d, s, b, G)
            return emit

        def l0b_sp(sp):
            def emit(k, r):
                for s, b in steps_at(k, r, 7, NS):
                    sp.wait_ge(sum_sb.sem, sum_sb.at(s))
                    sp.sem_inc(sp_fence, 1)
                    sp.dma_start(a1_v[s], OUT[:, b]).then_inc(stored2.sem(b), 16)
                for s, b in steps_at(k, r, 1, NS):
                    if begun(s - 4):
                        sp.wait_ge(prod_sb.sem, prod_sb.at(s - 4))
                        sp.sem_inc(sp_fence, 1)
                    sp.dma_start(L0[:, b], xs_v[s]).then_inc(fetched.sem(b), 16)
                for s, b in steps_at(k, r, 5, NS):
                    sp.wait_ge(prod_sb.sem, prod_sb.at(s))
                    sp.sem_inc(sp_fence, 1)
                    sp.dma_start(x1s_v[s], XE[:, b, :, 0:F]).then_inc(stored.sem(b), 16)
            return emit

        def l0b_act(act):
            def emit(k, r):
                for s, b in steps_at(k, r, 4, NS):
                    hidden_act(act, s, b)
                for s, b in steps_at(k, r, 6, NS):
                    carry(act, s, b, F)
                for s, b in steps_at(k, r, 2, NS):
                    root(act, ln_made, rooted, s, emv[0][:, b % 2], ers[0][:, b % 2], 128, 0)
                    act.wait_ge(ln_made.sem, ln_made.at(s))
                    if begun(s - 2):
                        act.wait_ge(turned.sem, turned.at(s - 2))
                    relu_norm(act, h_made, h[:, b % 2], L0[:, b], ers[0][:, b % 2], enm[0][:, b % 2], 128, J)
            return emit

        def l0b_pe(pe):
            def emit(k, r):
                for s, b in steps_at(k, r, 5, NS):
                    product_pe(pe, s, b, True)
                for s, b in steps_at(k, r, 3, NS):
                    pe.wait_ge(gathered.sem(b), gathered.at(s, b))
                    turn_pe(pe, s, b, G)
                for s, b in steps_at(k, r, 4, NS):
                    hidden_pe(pe, s, b)
                for s, b in steps_at(k, r, 6, NS):
                    sum_segments(pe, s, b, F)
            return emit

        run_phase(LAG, {"vector": l0b_dve, "gpsimd": l0b_pool, "sync": l0b_sp, "scalar": l0b_act, "tensor": l0b_pe,
                        "sync_end": [all_stored(stored), all_stored(stored2)]}, 104,
                  beside=mark_rows(by_s, has_out))
        mark_ready.close(2 * NS), marked.close(NS)
        assert dense_at[0] == ND + DLAG
        idx_ready.close(NS), gathered.close(NS), fetched.close(NS), stored.close(NS), stored2.close(NS)
        ln_made.close(4 * NS), rooted.close(NS), msg_made.close(NS), sum_sb.close(NS), h_made.close(NS), turned.close(NS)
        turned_sb.close(NS), hid_ps.close(2 * NS), hid_sb.close(2 * NS)
        prod_ps.close(NS), prod_sb.close(2 * NS)
        close_sums()

        LAG = 10
        fetched.open(2), prod_sb.open(3), ln2_made.open(4), rooted2.open(1), h2_made.open(1), turned_b.open(1), turned_b_sb.open(1)
        prod_b_ps.open(1), msg_made.open(1), same_made.open(3), sum_sb.open(1)
        x1d_v, qe_v = by_step(x1d_d), by_step(qe_d)

        def l1q_dve(dve):
            def emit(k, r):
                for s, b in steps_at(k, r, 10, NS):
                    sums_ready(dve, s)
                    if begun(s - 4):
                        dve.wait_ge(stored2.sem(b), stored2.at(s - 4, b))
                    dve.tensor_copy(OUT[:, b], jview(SS[:, 0:W])).then_inc(sum_sb.sem, 1)
                for s, b in steps_at(k, r, 0, NS):
                    nodes = by_d.key_g[:, bass.ds(J * (NS - 1 - s), J)]
                    if begun(s - UNROLL):
                        dve.wait_ge(gathered.sem(b), gathered.at(s - UNROLL, b))
                        dve.sem_inc(dve_fence, 1)
                    dve.tensor_copy(idx[:, b, :], nodes).then_inc(idx_ready.sem, 1)
                for s, b in steps_at(k, r, 8, NS):
                    q = NS - 1 - s
                    q_keys = key_q[:, bass.ds(J * q, J), 1:128]
                    row_keys = by_d.key_r[:, bass.ds(J * q, J)].unsqueeze(2).to_broadcast([128, J, 127])
                    row_reps = by_d.rep_r[:, bass.ds(J * q, J)].unsqueeze(2).to_broadcast([128, J, 127])
                    if begun(s - 2):
                        dve.wait_ge(sum_ps.sem, sum_ps.at(s - 2))
                        dve.sem_inc(dve_fence, 1)
                    dve.tensor_tensor(S[:, b % 2, :, 1:128], q_keys,
                                      row_keys, ALU.is_equal).then_inc(same_made.sem, 1)
                    dve.wait_ge(same_made.sem, same_made.at(s, 1))
                    dve.tensor_tensor(S[:, b % 2, :, 1:128], S[:, b % 2, :, 1:128],
                                      row_reps, ALU.mult).then_inc(same_made.sem, 1)
                    dve.wait_ge(same_made.sem, same_made.at(s, 2))
                    dve.tensor_copy(S[:, b % 2, :, 0:1], S[:, b % 2, :, 1:2]).then_inc(same_made.sem, 1)
                for s, b in steps_at(k, r, 5, NS):
                    dve.wait_ge(fetched.sem(b), fetched.at(s, b))
                    if begun(s - 4):
                        dve.wait_ge(stored.sem(b), stored.at(s - 4, b))
                    if begun(s - 4):
                        dve.wait_ge(h2_made.sem, h2_made.at(s - 4))
                    dve.tensor_tensor(XE[:, b, :, 0:F], G[:, b], L[:, b, 1, :, :], ALU.add).then_inc(prod_sb.sem, 1)
                    dve.wait_ge(prod_sb.sem, prod_sb.at(s, 1))
                    dve.tensor_tensor(XE[:, b, :, 0:F], XE[:, b, :, 0:F],
                                      b2[:, :].unsqueeze(1).to_broadcast([128, J, F]), ALU.add) \
                        .then_inc(prod_sb.sem, 1)
                    dve.wait_ge(prod_sb.sem, prod_sb.at(s, 2))
                    dve.wait_ge(prod_ps.sem, prod_ps.at(s))
                    dve.tensor_tensor(XE[:, b, :, 0:F], XE[:, b, :, 0:F], jview(SB[:, 0:W]), ALU.add) \
                        .then_inc(prod_sb.sem, 1)
                for s, b in steps_at(k, r, 8, NS):
                    dve.wait_ge(prod_b_ps.sem, prod_b_ps.at(s))
                    if begun(s - 2):
                        dve.wait_ge(sum_ps.sem, sum_ps.at(s - 2))
                    if begun(s - 2):
                        dve.wait_ge(carried.sem, carried.at(s - 2))
                    dve.tensor_tensor(M[:, b % 2, :, 0:F], jview(bank[1][:, 0:W]),
                                      bq[:, :].unsqueeze(1).to_broadcast([128, J, F]), ALU.add) \
                        .then_inc(msg_made.sem, 1)
                for s, b in steps_at(k, r, 3, NS):
                    turned_dve(dve, s, b)
                for s, b in steps_at(k, r, 2, NS):
                    dve.wait_ge(gathered.sem(b), gathered.at(s, b))
                    if begun(s - 2):
                        dve.wait_ge(h_made.sem, h_made.at(s - 2))
                    ln_stats(dve, ln_made, s, G[:, b], est[0][:, b % 2], emv[0][:, b % 2], 128, J, 0)
                for s, b in steps_at(k, r, 6, NS):
                    dve.wait_ge(prod_sb.sem, prod_sb.at(s))
                    if begun(s - 2):
                        dve.wait_ge(h2_made.sem, h2_made.at(s - 2))
                    ln_stats(dve, ln2_made, s, XE[:, b, :, 0:F], est[1][:, b % 2], emv[1][:, b % 2], 128, J, 0)
                for s, b in steps_at(k, r, 2, NS):
                    ln_scale(dve, ln_made, rooted, s, emv[0][:, b % 2], ers[0][:, b % 2], enm[0][:, b % 2], 128, 0)
                for s, b in steps_at(k, r, 6, NS):
                    ln_scale(dve, ln2_made, rooted2, s, emv[1][:, b % 2], ers[1][:, b % 2], enm[1][:, b % 2], 128, 0)
            return emit

        def l1q_pool(pool):
            def emit(k, r):
                for s, b in steps_at(k, r, 1, NS):
                    pool.wait_ge(idx_ready.sem, idx_ready.at(s))
                    pool.sem_inc(pool_fence, 1)
                    if begun(s - 4):
                        pool.wait_ge(prod_sb.sem, prod_sb.at(s - 4))
                        pool.sem_inc(pool_fence, 1)
                    if begun(s - 4):
                        pool.wait_ge(h_made.sem, h_made.at(s - 4))
                        pool.sem_inc(pool_fence, 1)
                    gather(pool, d["x"], s, b, G)
            return emit

        def l1q_sp(sp):
            def emit(k, r):
                for s, b in steps_at(k, r, 10, NS):
                    sp.wait_ge(sum_sb.sem, sum_sb.at(s))
                    sp.sem_inc(sp_fence, 1)
                    sp.dma_start(qe_v[NS - 1 - s], OUT[:, b]).then_inc(stored2.sem(b), 16)
                for s, b in steps_at(k, r, 1, NS):
                    q = NS - 1 - s
                    if begun(s - 4):
                        sp.wait_ge(prod_sb.sem, prod_sb.at(s - 4))
                        sp.sem_inc(sp_fence, 1)
                    if begun(s - 4):
                        sp.wait_ge(turned.sem, turned.at(s - 4))
                        sp.sem_inc(sp_fence, 1)
                    sp.dma_start(L[:, b, 0, :, :], a0_v[q]).then_inc(fetched.sem(b), 16)
                    sp.dma_start(L[:, b, 1, :, :], a1_v[q]).then_inc(fetched.sem(b), 16)
                for s, b in steps_at(k, r, 5, NS):
                    sp.wait_ge(prod_sb.sem, prod_sb.at(s))
                    sp.sem_inc(sp_fence, 1)
                    sp.dma_start(x1d_v[NS - 1 - s], XE[:, b, :, 0:F]).then_inc(stored.sem(b), 16)
            return emit

        def l1q_act(act):
            act.activation(M[:, 0, J - 1, 0:F], ident[:, :], ACT.Copy)

            def emit(k, r):
                for s, b in steps_at(k, r, 7, NS):
                    act.wait_ge(turned_b.sem, turned_b.at(s))
                    if begun(s - 2):
                        act.wait_ge(prod_b_ps.sem, prod_b_ps.at(s - 2))
                    act.activation(hbT[:, b % 2, :], bank[0][:, 0:W], ACT.Copy).then_inc(turned_b_sb.sem, 1)
                for s, b in steps_at(k, r, 4, NS):
                    hidden_act(act, s, b)
                for s, b in steps_at(k, r, 9, NS):
                    for j in reversed(range(J)):
                        if isinstance(s, int) and s == NS - 1 and j == 0:
                            continue
                        act.wait_ge(sum_ps.sem, sum_ps.at(s, J - j))
                        nb, nj = (b % 2, j - 1) if j else ((b + 1) % 2, J - 1)
                        if j == 0:
                            act.wait_ge(msg_made.sem, msg_made.at(s + 1))
                        act.activation(M[0:1, nb, nj, 0:F], SS[0:1, j * F:(j + 1) * F], ACT.Copy) \
                            .then_inc(carried.sem, 1)
                for s, b in steps_at(k, r, 2, NS):
                    root(act, ln_made, rooted, s, emv[0][:, b % 2], ers[0][:, b % 2], 128, 0)
                for s, b in steps_at(k, r, 6, NS):
                    root(act, ln2_made, rooted2, s, emv[1][:, b % 2], ers[1][:, b % 2], 128, 0)
                for s, b in steps_at(k, r, 2, NS):
                    act.wait_ge(ln_made.sem, ln_made.at(s))
                    if begun(s - 2):
                        act.wait_ge(turned.sem, turned.at(s - 2))
                    relu_norm(act, h_made, h[:, b % 2], G[:, b], ers[0][:, b % 2], enm[0][:, b % 2], 128, J)
                for s, b in steps_at(k, r, 6, NS):
                    act.wait_ge(ln2_made.sem, ln2_made.at(s))
                    if begun(s - 2):
                        act.wait_ge(turned_b.sem, turned_b.at(s - 2))
                    relu_norm(act, h2_made, hb[:, b % 2], XE[:, b, :, 0:F], ers[1][:, b % 2], enm[1][:, b % 2], 128, J)
            return emit

        def l1q_pe(pe):
            def emit(k, r):
                for s, b in steps_at(k, r, 5, NS):
                    product_pe(pe, s, b, False)
                for s, b in steps_at(k, r, 8, NS):
                    pe.wait_ge(turned_b_sb.sem, turned_b_sb.at(s))
                    if begun(s - 1):
                        pe.wait_ge(msg_made.sem, msg_made.at(s - 1))
                    for j in range(J):
                        last = pe.matmul(bank[1][:, j * F:(j + 1) * F], hbT[:, b % 2, j * 128:(j + 1) * 128],
                                         wq[:, :], start=True, stop=True)
                    last.then_inc(prod_b_ps.sem, 1)
                for s, b in steps_at(k, r, 3, NS):
                    pe.wait_ge(fetched.sem(b), fetched.at(s, b))
                    turn_pe(pe, s, b, L0)
                for s, b in steps_at(k, r, 7, NS):
                    pe.wait_ge(h2_made.sem, h2_made.at(s))
                    if begun(s - 1):
                        pe.wait_ge(turned_b_sb.sem, turned_b_sb.at(s - 1))
                    for j in range(J):
                        last = pe.transpose(bank[0][:, j * 128:(j + 1) * 128], hb[:, b % 2, j, :], ident[:, :])
                    last.then_inc(turned_b.sem, 1)
                for s, b in steps_at(k, r, 4, NS):
                    hidden_pe(pe, s, b)
                for s, b in steps_at(k, r, 9, NS):
                    pe.wait_ge(same_made.sem, same_made.at(s))
                    pe.wait_ge(msg_made.sem, msg_made.at(s))
                    if begun(s - 1):
                        pe.wait_ge(sum_sb.sem, sum_sb.at(s - 1))
                    for n, j in enumerate(reversed(range(J))):
                        if not (isinstance(s, int) and J * s + n == 0):
                            pe.wait_ge(carried.sem, carried.at(s, n))
                        pe.matmul(SS[:, j * F:(j + 1) * F], S[:, b % 2, j, :], M[:, b % 2, j, 0:F],
                                  start=True, stop=True).then_inc(sum_ps.sem, 1)
            return emit

        run_phase(LAG, {"vector": l1q_dve, "gpsimd": l1q_pool, "sync": l1q_sp, "scalar": l1q_act, "tensor": l1q_pe,
                        "sync_end": [all_stored(stored), all_stored(stored2), all_stored(x_out, ND)]}, 10 ** 6)
        idx_ready.close(NS), gathered.close(NS), fetched.close(NS), stored.close(NS), stored2.close(NS)
        ln_made.close(4 * NS), rooted.close(NS), ln2_made.close(4 * NS), rooted2.close(NS), msg_made.close(NS), sum_sb.close(NS), h_made.close(NS)
        h2_made.close(NS), turned.close(NS), turned_sb.close(NS), hid_ps.close(2 * NS)
        hid_sb.close(2 * NS), prod_ps.close(NS), prod_sb.close(3 * NS), turned_b.close(NS), turned_b_sb.close(NS)
        prod_b_ps.close(NS)
        same_made.close(3 * NS), sum_ps.close(J * NS), carried.close(T - 1)

        LAG = 8
        ln_made.open(5), rooted.open(1), h_made.open(1), turned.open(1), turned_sb.open(1), prod_ps.open(1), prod_sb.open(9)
        exp_made.open(1), msg_made.open(1), same_made.open(1), sum_sb.open(4), fetched.open(2), fetched2.open(1)
        idx_ready2.open(1), scattered.open(J)
        KB, EB, VB = aT, hid[:, :, 0, :], hid[:, :, 1, :]

        def l1_dve(dve):
            def emit(k, r):
                for s, b in steps_at(k, r, 7, NS):
                    sums_ready(dve, s)
                    dve.wait_ge(fetched2.sem(b), fetched2.at(s, b))
                    if begun(s - 4):
                        dve.wait_ge(scattered.sem(b), scattered.at(s - 4, b))
                    dve.tensor_scalar(nrm[:, b % 2], SS4[:, :, F:F + HEADS], Z_EPS, None, ALU.add) \
                        .then_inc(sum_sb.sem, 1)
                    dve.wait_ge(sum_sb.sem, sum_sb.at(s, 1))
                    dve.reciprocal(nrm[:, b % 2], nrm[:, b % 2]).then_inc(sum_sb.sem, 1)
                    dve.wait_ge(sum_sb.sem, sum_sb.at(s, 2))
                    dve.tensor_tensor(OUT[:, b].rearrange("p j (h c) -> p j h c", h=HEADS),
                                      SS4[:, :, 0:F].rearrange("p j (h c) -> p j h c", h=HEADS),
                                      nrm[:, b % 2].unsqueeze(3).to_broadcast([128, J, HEADS, HD]), ALU.mult) \
                        .then_inc(sum_sb.sem, 1)
                    dve.wait_ge(sum_sb.sem, sum_sb.at(s, 3))
                    dve.tensor_tensor(OUT[:, b], OUT[:, b], L[:, b, 2, :, :], ALU.add).then_inc(sum_sb.sem, 1)
                    dve.tensor_copy(idx2[:, b, :], by_d.key_s[:, bass.ds(J * s, J)]).then_inc(idx_ready2.sem, 1)
                for s, b in steps_at(k, r, 0, NS):
                    if begun(s - UNROLL):
                        dve.wait_ge(gathered.sem(b), gathered.at(s - UNROLL, b))
                    dve.sem_inc(dve_fence, 1)
                    dve.tensor_copy(idx[:, b, :], ss_i[:, bass.ds(J * s, J)]).then_inc(idx_ready.sem, 1)
                for s, b in steps_at(k, r, 5, NS):
                    build_same(dve, s, b)
                for s, b in steps_at(k, r, 4, NS):
                    kb, eb, vb = jview(KB[:, b % 2, :]), jview(EB[:, b % 2, :]), jview(VB[:, b % 2, :])
                    dve.wait_ge(prod_ps.sem, prod_ps.at(s))
                    dve.tensor_tensor(kb, SB4[:, :, 0:F], bkv[:, 0:F].unsqueeze(1).to_broadcast([128, J, F]),
                                      ALU.add).then_inc(prod_sb.sem, 1)
                    dve.tensor_tensor(eb, we[:, :].unsqueeze(1).to_broadcast([128, J, F]),
                                      by_d.w[:, bass.ds(J * s, J)].unsqueeze(2).to_broadcast([128, J, F]),
                                      ALU.mult).then_inc(prod_sb.sem, 1)
                    dve.wait_ge(prod_sb.sem, prod_sb.at(s, 1))
                    dve.tensor_tensor(kb, kb, L[:, b, 1, :, :], ALU.mult).then_inc(prod_sb.sem, 1)
                    dve.wait_ge(prod_sb.sem, prod_sb.at(s, 2))
                    dve.tensor_tensor(eb, eb, be[:, :].unsqueeze(1).to_broadcast([128, J, F]), ALU.add) \
                        .then_inc(prod_sb.sem, 1)
                    if begun(s - 2):
                        dve.wait_ge(msg_made.sem, msg_made.at(s - 2))
                    dve.tensor_tensor(vb, SB4[:, :, F:2 * F], bkv[:, F:2 * F].unsqueeze(1).to_broadcast([128, J, F]),
                                      ALU.add).then_inc(prod_sb.sem, 1)
                    dve.wait_ge(prod_sb.sem, prod_sb.at(s, 4))
                    dve.tensor_tensor(kb, kb, eb, ALU.mult).then_inc(prod_sb.sem, 1)
                    dve.wait_ge(prod_sb.sem, prod_sb.at(s, 6))
                    if begun(s - 2):
                        dve.wait_ge(exp_made.sem, exp_made.at(s - 2))
                    dve.tensor_reduce(sc[:, b % 2].rearrange("p j h -> p (j h)"),
                                      KB[:, b % 2, :].rearrange("p (a c) -> p a c", c=HD), AX.X, ALU.add) \
                        .then_inc(prod_sb.sem, 1)
                    dve.wait_ge(prod_sb.sem, prod_sb.at(s, 7))
                    dve.tensor_scalar(sc[:, b % 2], sc[:, b % 2], HD ** -0.5, -5.0, ALU.mult, ALU.max) \
                        .then_inc(prod_sb.sem, 1)
                    dve.wait_ge(prod_sb.sem, prod_sb.at(s, 8))
                    dve.tensor_scalar(sc[:, b % 2], sc[:, b % 2], 5.0, None, ALU.min).then_inc(prod_sb.sem, 1)
                for s, b in steps_at(k, r, 5, NS):
                    vb = jview(VB[:, b % 2, :])
                    dve.wait_ge(exp_made.sem, exp_made.at(s))
                    dve.tensor_tensor(M[:, b % 2, :, 0:F].rearrange("p j (h c) -> p j h c", h=HEADS),
                                      vb.rearrange("p j (h c) -> p j h c", h=HEADS),
                                      M[:, b % 2, :, F:F + HEADS].unsqueeze(3).to_broadcast([128, J, HEADS, HD]),
                                      ALU.mult).then_inc(msg_made.sem, 1)
                for s, b in steps_at(k, r, 2, NS):
                    dve.wait_ge(gathered.sem(b), gathered.at(s, b))
                    dve.wait_ge(fetched.sem(b), fetched.at(s, b))
                    if begun(s - 2):
                        dve.wait_ge(h_made.sem, h_made.at(s - 2))
                    dve.tensor_tensor(XE[:, b, :, 0:F], L[:, b, 0, :, :], G[:, b], ALU.add).then_inc(ln_made.sem, 1)
                    dve.wait_ge(ln_made.sem, ln_made.at(s, 1))
                    ln_stats(dve, ln_made, s, XE[:, b, :, 0:F], est[0][:, b % 2], emv[0][:, b % 2], 128, J, 1)
                for s, b in steps_at(k, r, 2, NS):
                    ln_scale(dve, ln_made, rooted, s, emv[0][:, b % 2], ers[0][:, b % 2], enm[0][:, b % 2], 128, 1)
            return emit

        def l1_pool(pool):
            def emit(k, r):
                for s, b in steps_at(k, r, 1, NS):
                    pool.wait_ge(idx_ready.sem, idx_ready.at(s))
                    pool.sem_inc(pool_fence, 1)
                    if begun(s - 4):
                        pool.wait_ge(ln_made.sem, ln_made.at(s - 4))
                        pool.sem_inc(pool_fence, 1)
                    gather(pool, a1_d, s, b, G)
                for s, b in steps_at(k, r, 8, NS):
                    pool.wait_ge(idx_ready2.sem, idx_ready2.at(s))
                    pool.sem_inc(pool_fence, 1)
                    pool.wait_ge(sum_sb.sem, sum_sb.at(s))
                    pool.sem_inc(pool_fence, 1)
                    for j in range(J):
                        pool.indirect_dma_start(
                            x2_d, bass.IndirectOffsetOnAxis(ap=idx2[:, b, j:j + 1], axis=0), OUT[:, b, j, :], None,
                            bounds_check=N - 1, oob_is_err=False).then_inc(scattered.sem(b), 16)
            return emit

        def l1_sp(sp):
            def emit(k, r):
                for s, b in steps_at(k, r, 1, NS):
                    if begun(s - 4):
                        sp.wait_ge(prod_sb.sem, prod_sb.at(s - 4))
                        sp.sem_inc(sp_fence, 1)
                    sp.dma_start(L[:, b, 0, :, :], x1s_v[s]).then_inc(fetched.sem(b), 16)
                    sp.dma_start(L[:, b, 1, :, :], qe_v[s]).then_inc(fetched.sem(b), 16)
                for s, b in steps_at(k, r, 5, NS):
                    if begun(s - 4):
                        sp.wait_ge(sum_sb.sem, sum_sb.at(s - 4))
                        sp.sem_inc(sp_fence, 1)
                    sp.dma_start(L[:, b, 2, :, :], x1d_v[s]).then_inc(fetched2.sem(b), 16)
            return emit

        def l1_act(act):
            def emit(k, r):
                for s, b in steps_at(k, r, 5, NS):
                    act.wait_ge(prod_sb.sem, prod_sb.at(s))
                    if begun(s - 2):
                        act.wait_ge(sum_ps.sem, sum_ps.at(s - 2))
                    act.activation(M[:, b % 2, :, F:F + HEADS], sc[:, b % 2], ACT.Exp).then_inc(exp_made.sem, 1)
                for s, b in steps_at(k, r, 3, NS):
                    act.wait_ge(turned.sem, turned.at(s))
                    if begun(s - 2):
                        act.wait_ge(prod_ps.sem, prod_ps.at(s - 2))
                    act.activation(hT[:, b % 2, :], ST[:, 0:W], ACT.Copy).then_inc(turned_sb.sem, 1)
                for s, b in steps_at(k, r, 6, NS):
                    carry(act, s, b, F + HEADS)
                for s, b in steps_at(k, r, 2, NS):
                    root(act, ln_made, rooted, s, emv[0][:, b % 2], ers[0][:, b % 2], 128, 1)
                    act.wait_ge(ln_made.sem, ln_made.at(s))
                    if begun(s - 2):
                        act.wait_ge(turned.sem, turned.at(s - 2))
                    relu_norm(act, h_made, h[:, b % 2], XE[:, b, :, 0:F], ers[0][:, b % 2], enm[0][:, b % 2], 128, J)
            return emit

        def l1_pe(pe):
            def emit(k, r):
                for s, b in steps_at(k, r, 4, NS):
                    pe.wait_ge(turned_sb.sem, turned_sb.at(s))
                    if begun(s - 1):
                        pe.wait_ge(prod_sb.sem, prod_sb.at(s - 1))
                    for j in range(J):
                        last = pe.matmul(SB4[:, j, :], hT[:, b % 2, j * 128:(j + 1) * 128], wkv[:, :],
                                         start=True, stop=True)
                    last.then_inc(prod_ps.sem, 1)
                for s, b in steps_at(k, r, 3, NS):
                    pe.wait_ge(h_made.sem, h_made.at(s))
                    if begun(s - 1):
                        pe.wait_ge(turned_sb.sem, turned_sb.at(s - 1))
                    for j in range(J):
                        last = pe.transpose(ST[:, j * 128:(j + 1) * 128], h[:, b % 2, j, :], ident[:, :])
                    last.then_inc(turned.sem, 1)
                for s, b in steps_at(k, r, 6, NS):
                    sum_segments(pe, s, b, F + HEADS)
            return emit

        run_phase(LAG, {"vector": l1_dve, "gpsimd": l1_pool, "sync": l1_sp, "scalar": l1_act, "tensor": l1_pe,
                        "gpsimd_end": [all_stored(scattered)]})
        idx_ready.close(NS), idx_ready2.close(NS), gathered.close(NS), fetched.close(NS), fetched2.close(NS), scattered.close(NS)
        ln_made.close(5 * NS), rooted.close(NS), msg_made.close(NS), sum_sb.close(4 * NS), h_made.close(NS)
        turned.close(NS), turned_sb.close(NS), prod_ps.close(NS), prod_sb.close(9 * NS), exp_made.close(NS)
        close_sums()

        tables[0] = by_s
        x_in.close(ND)
        marks = no_out[:, :].bitcast(i32)
        with nc.Block() as block:
            @block.sync
            def _(sp):
                full = GR * NF
                sp.dma_start(marks[:, 0:J * NF].rearrange("p (g j) -> p g j", j=J),
                             has_out[0:full, :].rearrange("(g p j) a -> p g (j a)", p=128, j=J)) \
                    .then_inc(setup_dma.sem, 16)
                if TAIL:
                    sp.dma_start(marks[0:TAIL, J * NF:J * ND],
                                 has_out[full:N, :].rearrange("(p j) a -> p (j a)", j=J)).then_inc(setup_dma.sem, 16)
                load_key_q(sp, by_src["key"])

            @block.vector
            def _(dve):
                dve.wait_ge(setup_dma.sem, setup_dma.base + 16 + 16 * (TAIL > 0))
                dve.tensor_scalar(no_out[:, 0:J * NF], marks[:, 0:J * NF], float(C), None, ALU.is_equal)
                if TAIL:
                    dve.tensor_scalar(no_out[0:TAIL, J * NF:], marks[0:TAIL, J * NF:], float(C), None, ALU.is_equal)
                make_key_q(dve)
        setup_dma.close(16 + 16 * (TAIL > 0)), loaded.close(16 * QC)

        LAG = 8
        idx_ready.open(2), stored.open(1), stored2.open(1), fetched.open(1), gathered.open(2 * J), ln_made.open(4), rooted.open(1), ln2_made.open(5), rooted2.open(1), h2_made.open(1), turned.open(1)
        turned_sb.open(1), prod_ps.open(1), prod_sb.open(1), hid_sb.open(1), turned_b.open(1), turned_b_sb.open(1)
        sum_sb.open(2)
        xyd_v = by_step(xyd_d)
        HP = hid[:, :, 0, :]

        def l2_dve(dve):
            def emit(k, r):
                for s, b in steps_at(k, r, 5, NS):
                    sums_ready(dve, s)
                    if begun(s - 2):
                        dve.wait_ge(turned.sem, turned.at(s - 2))
                    hp = jview(HP[:, b % 2, :])
                    dve.tensor_tensor(hp, SS4[:, :, 0:F],
                                      by_s.is_rep[:, bass.ds(J * s, J)].unsqueeze(2).to_broadcast([128, J, F]), ALU.mult) \
                        .then_inc(sum_sb.sem, 1)
                    dve.wait_ge(sum_sb.sem, sum_sb.at(s, 1))
                    dve.wait_ge(h2_made.sem, h2_made.at(s))
                    dve.scalar_tensor_tensor(out=HP[:, b % 2, :], in0=h[:, b % 2].rearrange("p j f -> p (j f)"),
                                             scalar=cols[:, 7:8], in1=HP[:, b % 2, :], op0=ALU.mult, op1=ALU.add) \
                        .then_inc(sum_sb.sem, 1)
                for s, b in steps_at(k, r, 0, NS):
                    if begun(s - UNROLL):
                        dve.wait_ge(gathered.sem(b), gathered.at(s - UNROLL, b))
                    dve.sem_inc(dve_fence, 1)
                    dve.tensor_copy(idx[:, b, :], by_s.other[:, bass.ds(J * s, J)]).then_inc(idx_ready.sem, 1)
                    dve.tensor_copy(idx2[:, b, :], by_s.key_g[:, bass.ds(J * s, J)]).then_inc(idx_ready.sem, 1)
                for s, b in steps_at(k, r, 3, NS):
                    build_same(dve, s, b)
                for s, b in steps_at(k, r, 8, NS):
                    dve.wait_ge(hid_sb.sem, hid_sb.at(s))
                    dve.sem_inc(dve_fence, 1)
                    dve.bn_stats(ystat[:, bass.ds(ND + s, 1), :].rearrange("p a c -> p (a c)"), aT[:, b % 2, :]) \
                        .then_inc(prod_sb.sem, 1)
                for s, b in steps_at(k, r, 2, NS):
                    dve.wait_ge(gathered.sem(b), gathered.at(s, b))
                    if begun(s - 2):
                        dve.wait_ge(msg_made.sem, msg_made.at(s - 2))
                    ln_stats(dve, ln_made, s, G[:, b], est[0][:, b % 2], emv[0][:, b % 2], 128, J, 0)
                for s, b in steps_at(k, r, 3, NS):
                    if begun(s - 2):
                        dve.wait_ge(h2_made.sem, h2_made.at(s - 2))
                    ln_stats(dve, ln2_made, s, XE[:, b, :, 0:F], est[1][:, b % 2], emv[1][:, b % 2], 128, J, 0)
                for s, b in steps_at(k, r, 2, NS):
                    ln_scale(dve, ln_made, rooted, s, emv[0][:, b % 2], ers[0][:, b % 2], enm[0][:, b % 2], 128, 0)
                for s, b in steps_at(k, r, 3, NS):
                    ln_scale(dve, ln2_made, rooted2, s, emv[1][:, b % 2], ers[1][:, b % 2], enm[1][:, b % 2], 128, 0,
                             mask=by_s.is_rep[:, bass.ds(J * s, J)])
            return emit

        def l2_pool(pool):
            def emit(k, r):
                for s, b in steps_at(k, r, 1, NS):
                    pool.wait_ge(idx_ready.sem, idx_ready.at(s))
                    pool.sem_inc(pool_fence, 1)
                    if begun(s - 4):
                        pool.wait_ge(msg_made.sem, msg_made.at(s - 4))
                        pool.sem_inc(pool_fence, 1)
                    if begun(s - 4):
                        pool.wait_ge(h2_made.sem, h2_made.at(s - 4))
                        pool.sem_inc(pool_fence, 1)
                    if begun(s - 4):
                        pool.wait_ge(stored.sem(b), stored.at(s - 4, b))
                        pool.sem_inc(pool_fence, 1)
                    gather(pool, x2_d, s, b, G)
                    for j in range(J):
                        pool.indirect_dma_start(XE[:, b, j, 0:F], None, x2_d,
                                                bass.IndirectOffsetOnAxis(ap=idx2[:, b, j:j + 1], axis=0)) \
                            .then_inc(gathered.sem(b), 16)
            return emit

        def l2_sp(sp):
            def emit(k, r):
                for s, b in steps_at(k, r, 2, NS):
                    sp.wait_ge(gathered.sem(b), gathered.at(s, b))
                    sp.sem_inc(sp_fence, 1)
                    sp.dma_start(xyd_v[s][:, :, 0:F], XE[:, b, :, 0:F]).then_inc(stored.sem(b), 16)
                for s, b in steps_at(k, r, 8, NS):
                    sp.wait_ge(turned_b_sb.sem, turned_b_sb.at(s))
                    sp.sem_inc(sp_fence, 1)
                    sp.dma_start(xyd_v[s][:, :, F:2 * F], XE[:, b, :, F:2 * F]).then_inc(stored2.sem(b), 16)
            return emit

        def l2_act(act):
            def emit(k, r):
                for s, b in steps_at(k, r, 6, NS):
                    act.wait_ge(turned.sem, turned.at(s))
                    if begun(s - 2):
                        act.wait_ge(prod_ps.sem, prod_ps.at(s - 2))
                    act.activation(hT[:, b % 2, :], ST[:, 0:W], ACT.Copy).then_inc(turned_sb.sem, 1)
                for s, b in steps_at(k, r, 8, NS):
                    if begun(s - 4):
                        act.wait_ge(stored2.sem(b), stored2.at(s - 4, b))
                    act.wait_ge(turned_b.sem, turned_b.at(s))
                    act.activation(XE[:, b, :, F:2 * F], jview(bank[3][:, 0:W]), ACT.Copy).then_inc(turned_b_sb.sem, 1)
                for s, b in steps_at(k, r, 7, NS):
                    act.wait_ge(prod_ps.sem, prod_ps.at(s))
                    if begun(s - 2):
                        act.wait_ge(turned_b.sem, turned_b.at(s - 2))
                    if begun(s - 2):
                        act.wait_ge(prod_sb.sem, prod_sb.at(s - 2))
                    act.activation(aT[:, b % 2, :], SB[:, 0:W], ACT.Copy).then_inc(hid_sb.sem, 1)
                for s, b in steps_at(k, r, 4, NS):
                    carry(act, s, b, F)
                for s, b in steps_at(k, r, 2, NS):
                    root(act, ln_made, rooted, s, emv[0][:, b % 2], ers[0][:, b % 2], 128, 0)
                for s, b in steps_at(k, r, 3, NS):
                    root(act, ln2_made, rooted2, s, emv[1][:, b % 2], ers[1][:, b % 2], 128, 0)
                for s, b in steps_at(k, r, 2, NS):
                    act.wait_ge(ln_made.sem, ln_made.at(s))
                    if begun(s - 2):
                        act.wait_ge(sum_ps.sem, sum_ps.at(s - 2))
                    if begun(s - 2):
                        act.wait_ge(carried.sem, carried.at(s - 2))
                    relu_norm(act, msg_made, M[:, b % 2, :, 0:F], G[:, b], ers[0][:, b % 2], enm[0][:, b % 2], 128, J)
                for s, b in steps_at(k, r, 3, NS):
                    act.wait_ge(ln2_made.sem, ln2_made.at(s))
                    if begun(s - 2):
                        act.wait_ge(sum_sb.sem, sum_sb.at(s - 2))
                    relu_norm(act, h2_made, h[:, b % 2], XE[:, b, :, 0:F], ers[1][:, b % 2], enm[1][:, b % 2], 128, J)
            return emit

        def l2_pe(pe):
            def emit(k, r):
                for s, b in steps_at(k, r, 6, NS):
                    pe.wait_ge(sum_sb.sem, sum_sb.at(s))
                    if begun(s - 1):
                        pe.wait_ge(turned_sb.sem, turned_sb.at(s - 1))
                    for j in range(J):
                        last = pe.transpose(ST[:, j * 128:(j + 1) * 128], HP[:, b % 2, j * 128:(j + 1) * 128],
                                            ident[:, :])
                    last.then_inc(turned.sem, 1)
                for s, b in steps_at(k, r, 8, NS):
                    pe.wait_ge(hid_sb.sem, hid_sb.at(s))
                    if begun(s - 1):
                        pe.wait_ge(turned_b_sb.sem, turned_b_sb.at(s - 1))
                    for j in range(J):
                        last = pe.transpose(bank[3][:, j * F:(j + 1) * F], aT[:, b % 2, j * 128:(j + 1) * 128],
                                            ident[:, :])
                    last.then_inc(turned_b.sem, 1)
                for s, b in steps_at(k, r, 7, NS):
                    pe.wait_ge(turned_sb.sem, turned_sb.at(s))
                    if begun(s - 1):
                        pe.wait_ge(hid_sb.sem, hid_sb.at(s - 1))
                    pe.matmul(SB[:, 0:W], w1[:, :], hT[:, b % 2, :], start=True, stop=True).then_inc(prod_ps.sem, 1)
                for s, b in steps_at(k, r, 4, NS):
                    sum_segments(pe, s, b, F)
            return emit

        run_phase(LAG, {"vector": l2_dve, "gpsimd": l2_pool, "sync": l2_sp, "scalar": l2_act, "tensor": l2_pe,
                        "sync_end": [all_stored(stored), all_stored(stored2), all_stored(y_out, ND)]}, 10 ** 6, dense_pass=1)
        idx_ready.close(2 * NS), gathered.close(NS), stored.close(NS), stored2.close(NS)
        ln_made.close(4 * NS), rooted.close(NS), ln2_made.close(5 * NS), rooted2.close(NS), msg_made.close(NS)
        sum_sb.close(2 * NS), h2_made.close(NS), turned.close(NS), turned_sb.close(NS), prod_ps.close(NS)
        prod_sb.close(NS), hid_sb.close(NS), turned_b.close(NS), turned_b_sb.close(NS)
        close_sums()

        def replace_rows(table, rows_v, buf):
            idx_ready.open(1), fetched.open(1), scattered.open(J)
            with nc.Block() as block:
                @block.sync
                def _(sp):
                    def emit(k, r):
                        for s, b in steps_at(k, r, 0, NS):
                            if begun(s - 4):
                                sp.wait_ge(scattered.sem(b), scattered.at(s - 4, b))
                                sp.sem_inc(sp_fence, 1)
                            sp.dma_start(buf[:, b, :, :], rows_v[s]).then_inc(fetched.sem(b), 16)
                    drive(sp, NS, [(emit, 0, (0, NS), (UNROLL, NS))])

                @block.vector
                def _(dve):
                    def emit(k, r):
                        for s, b in steps_at(k, r, 0, NS):
                            if begun(s - 4):
                                dve.wait_ge(scattered.sem(b), scattered.at(s - 4, b))
                            dve.sem_inc(dve_fence, 1)
                            dve.tensor_copy(idx[:, b, :], by_s.key_s[:, bass.ds(J * s, J)]).then_inc(idx_ready.sem, 1)
                    drive(dve, NS, [(emit, 0, (0, NS), (UNROLL, NS))])

                @block.gpsimd
                def _(pool):
                    def emit(k, r):
                        for s, b in steps_at(k, r, 0, NS):
                            pool.wait_ge(idx_ready.sem, idx_ready.at(s))
                            pool.sem_inc(pool_fence, 1)
                            pool.wait_ge(fetched.sem(b), fetched.at(s, b))
                            pool.sem_inc(pool_fence, 1)
                            for j in range(J):
                                pool.indirect_dma_start(
                                    table, bass.IndirectOffsetOnAxis(ap=idx[:, b, j:j + 1], axis=0),
                                    buf[:, b, j, :], None, bounds_check=N - 1, oob_is_err=False) \
                                    .then_inc(scattered.sem(b), 16)
                    drive(pool, NS, [(emit, 0, (0, NS), (UNROLL, NS))])
                    all_stored(scattered)(pool)
            idx_ready.close(NS), fetched.close(NS), scattered.close(NS)

        replace_rows(y_d, xyd_v[:, :, :, F:2 * F], OUT)

        def fold(dve, folded, mean_scale, mv, b_col, scale, offset):
            m, v, t, w = tiny[:, 2:3], tiny[:, 3:4], tiny[:, 4:5], tiny[:, 5:6]
            dve.tensor_scalar(m, mv[:, 0:1], mean_scale, None, ALU.mult).then_inc(zstep.sem, 1)
            dve.wait_ge(zstep.sem, zstep.next())
            dve.tensor_tensor(t, mv[:, 0:1], mv[:, 0:1], ALU.mult).then_inc(zstep.sem, 1)
            dve.wait_ge(zstep.sem, zstep.next())
            dve.tensor_tensor(v, mv[:, 1:2], t, ALU.add).then_inc(zstep.sem, 1)
            dve.wait_ge(zstep.sem, zstep.next())
            dve.tensor_scalar(v, v, mean_scale, None, ALU.mult).then_inc(zstep.sem, 1)
            dve.wait_ge(zstep.sem, zstep.next())
            dve.tensor_tensor(t, m, m, ALU.mult).then_inc(zstep.sem, 1)
            dve.wait_ge(zstep.sem, zstep.next())
            dve.tensor_tensor(v, v, t, ALU.subtract).then_inc(zstep.sem, 1)
            dve.wait_ge(zstep.sem, zstep.next())
            dve.tensor_scalar(v, v, 0.0, None, ALU.max).then_inc(zstep.sem, 1)
            dve.wait_ge(zstep.sem, zstep.next())
            folded()
            dve.reciprocal(v, v).then_inc(zstep.sem, 1)
            dve.wait_ge(zstep.sem, zstep.next())
            dve.tensor_tensor(scale, v, cols[:, b_col + 1:b_col + 2], ALU.mult).then_inc(zstep.sem, 1)
            dve.wait_ge(zstep.sem, zstep.next())
            dve.tensor_tensor(m, m, cols[:, b_col:b_col + 1], ALU.add).then_inc(zstep.sem, 1)
            dve.wait_ge(zstep.sem, zstep.next())
            dve.tensor_tensor(w, cols[:, b_col:b_col + 1], m, ALU.subtract).then_inc(zstep.sem, 1)
            dve.wait_ge(zstep.sem, zstep.next())
            dve.tensor_tensor(w, w, scale, ALU.mult).then_inc(zstep.sem, 1)
            dve.wait_ge(zstep.sem, zstep.next())
            dve.tensor_tensor(offset, w, cols[:, b_col + 2:b_col + 3], ALU.add).then_inc(zstep.sem, 1)
            dve.wait_ge(zstep.sem, zstep.next())

        zstep = sig("zstep")
        bn_rooted = sig("bn_rooted")
        W4 = J4 * 128
        y_in = slots("y_in").open(1)
        p_t = sig("p_t").open(1)
        p_a = sig("p_a").open(1)
        p_y = sig("p_y").open(1)
        p_s = sig("p_s").open(1)
        p_z = sig("p_z").open(1)
        p_b = sig("p_b").open(1)
        p_x = sig("p_x").open(1)
        y4, x4_groups = by_group(y_d, J4), by_group(x2_d, J4)
        out4 = by_group(out, J4)

        def rows4(s):
            return TAIL4 if isinstance(s, int) and s == NF4 else 128


        def through_act(dve, n):
            def wait_for_root():
                dve.wait_ge(bn_rooted.sem, n)
            return wait_for_root

        def bn_root(act, n, at):
            v = tiny[:, 3:4]
            act.wait_ge(zstep.sem, at)
            act.activation(v, v, ACT.Sqrt, bias=ln_eps[:, :]).then_inc(bn_rooted.sem, 1)

        yb = shared(0, 4, b=4, j=J4)
        xyb = shared(0, 8, b=4, j=J4)
        a1 = G[:, :, :, :].rearrange("p (b r) j f -> p b (r j f)", b=2)
        z2 = pair[:, :, :, :].rearrange("p b r w -> p b (r w)")
        with nc.Block() as block:
            @block.sync
            def _(sp):
                def emit(k, r):
                    for s, b in steps_at(k, r, 0, ND4):
                        P = rows4(s)
                        if begun(s - 4):
                            sp.wait_ge(p_t.sem, p_t.at(s - 4))
                            sp.sem_inc(sp_fence, 1)
                        sp.dma_start(yb[0:P, b], group(y4, s, NF4)) \
                            .then_inc(y_in.sem(b), 16)
                drive(sp, ND4, [(emit, 0, (0, ND4), (UNROLL, NF4))])

            @block.vector
            def _(dve):
                dve.bn_aggr(tiny[:, 0:2], ystat[:, :, :].rearrange("p a c -> p (a c)")).then_inc(zstep.sem, 1)
                dve.wait_ge(zstep.sem, zstep.next())
                fold(dve, through_act(dve, 1), (N + C) / N, tiny[:, 0:2], 0, bn[:, 0:1], bn[:, 1:2])

                def emit(k, r):
                    for s, b in steps_at(k, r, 3, ND4):
                        dve.wait_ge(p_y.sem, p_y.at(s))
                        dve.sem_inc(dve_fence, 1)
                        dve.bn_stats(ystat2[:, bass.ds(s, 1), :].rearrange("p a c -> p (a c)"),
                                     bank[2 + b % 2][:, 0:J4 * rows4(s)]).then_inc(p_s.sem, 1)
                drive(dve, ND4 + 3, [(emit, 0, (0, ND4 + 3), (2 * UNROLL, NF4))])
                dve.wait_ge(p_s.sem, p_s.at(ND4 - 1))
                dve.bn_aggr(tiny[:, 0:2], ystat2[:, 0:ND4, :].rearrange("p a c -> p (a c)")) \
                    .then_inc(zstep.sem, 1)
                dve.wait_ge(zstep.sem, zstep.next())
                fold(dve, through_act(dve, 2), 1.0, tiny[:, 0:2], 3, bn[:, 2:3], bn[:, 3:4])

            @block.scalar
            def _(act):
                bn_root(act, 1, 8)
                act.wait_ge(zstep.sem, 14)

                def emit(k, r):
                    for s, b in steps_at(k, r, 2, ND4):
                        P = rows4(s)
                        act.wait_ge(p_t.sem, p_t.at(s))
                        if begun(s - 2):
                            act.wait_ge(p_y.sem, p_y.at(s - 2))
                        act.activation(a1[:, b % 2, 0:J4 * P], bank[b % 2][:, 0:J4 * P], ACT.Relu,
                                       bias=bn[:, 1:2], scale=bn[:, 0:1]).then_inc(p_a.sem, 1)
                drive(act, ND4 + 3, [(emit, 0, (0, ND4 + 3), (2 * UNROLL, NF4))])
                bn_root(act, 2, 22)

            @block.tensor
            def _(pe):
                def emit(k, r):
                    for s, b in steps_at(k, r, 1, ND4):
                        P = rows4(s)
                        pe.wait_ge(y_in.sem(b), y_in.at(s, b))
                        if begun(s - 2):
                            pe.wait_ge(p_a.sem, p_a.at(s - 2))
                        for j in range(J4):
                            last = pe.transpose(bank[b % 2][:, j * P:(j + 1) * P], yb[0:P, b, j, :],
                                                ident[0:P, 0:P])
                        last.then_inc(p_t.sem, 1)
                    for s, b in steps_at(k, r, 3, ND4):
                        P = rows4(s)
                        pe.wait_ge(p_a.sem, p_a.at(s))
                        if begun(s - 2):
                            pe.wait_ge(p_s.sem, p_s.at(s - 2))
                        pe.matmul(bank[2 + b % 2][:, 0:J4 * P], w2[:, :], a1[:, b % 2, 0:J4 * P],
                                  start=True, stop=True).then_inc(p_y.sem, 1)
                drive(pe, ND4 + 3, [(emit, 0, (0, ND4 + 3), (2 * UNROLL, NF4))])
        y_in.close(ND4)
        p_t.close(ND4), p_a.close(ND4), p_y.close(ND4), p_s.close(ND4)

        with ExitStack() as ph:
            x3_out = slots("x3_out").open(1)
            x_in.close(ND)
            GX = XE

            def last_dense_sp(sp):
                def emit(k, r):
                    for s, b in steps_at(k, r, 0, ND4):
                        P = rows4(s)
                        if begun(s - 4):
                            sp.wait_ge(p_t.sem, p_t.at(s - 4))
                            sp.sem_inc(sp_fence, 1)
                        sp.dma_start(xyb[0:P, b, :, F:2 * F], group(y4, s, NF4)).then_inc(y_in.sem(b), 16)
                    for s, b in steps_at(k, r, 2, ND4):
                        P = rows4(s)
                        if begun(s - 4):
                            sp.wait_ge(p_x.sem, p_x.at(s - 4))
                            sp.sem_inc(sp_fence, 1)
                        sp.dma_start(xyb[0:P, b, :, 0:F], group(x4_groups, s, NF4)).then_inc(x_in.sem(b), 16)
                    for s, b in steps_at(k, r, 5, ND4):
                        P = rows4(s)
                        sp.wait_ge(p_x.sem, p_x.at(s))
                        sp.sem_inc(sp_fence, 1)
                        sp.dma_start(group(out4, s, NF4), x3_rows[0:P, b, :, :]).then_inc(x3_out.sem(b), 16)
                return emit

            def last_dense_act(act):
                def emit(k, r):
                    for s, b in steps_at(k, r, 2, ND4):
                        P = rows4(s)
                        act.wait_ge(p_t.sem, p_t.at(s))
                        if begun(s - 2):
                            act.wait_ge(p_y.sem, p_y.at(s - 2))
                        act.activation(a1[:, b % 2, 0:J4 * P], bank[0][:, 0:J4 * P], ACT.Relu,
                                       bias=bn[:, 1:2], scale=bn[:, 0:1]).then_inc(p_a.sem, 1)
                    for s, b in steps_at(k, r, 3, ND4):
                        P = rows4(s)
                        act.wait_ge(p_y.sem, p_y.at(s))
                        if begun(s - 2):
                            act.wait_ge(p_b.sem, p_b.at(s - 2))
                        act.activation(z2[:, b % 2, 0:J4 * P], bank[1][:, 0:J4 * P], ACT.Relu,
                                       bias=bn[:, 3:4], scale=bn[:, 2:3]).then_inc(p_z.sem, 1)
                return emit

            def last_dense_dve(dve):
                def emit(k, r):
                    for s, b in steps_at(k, r, 4, ND4):
                        P = rows4(s)
                        dve.wait_ge(p_b.sem, p_b.at(s))
                        dve.wait_ge(x_in.sem(b), x_in.at(s, b))
                        if begun(s - 4):
                            dve.wait_ge(x3_out.sem(b), x3_out.at(s - 4, b))
                        dve.tensor_tensor(x3_rows[0:P, b, :, :], xyb[0:P, b, :, 0:F],
                                          bank[2][0:P, :].rearrange("p (j f) -> p j f", j=J4), ALU.add) \
                            .then_inc(p_x.sem, 1)
                return emit

            def last_dense_pe(pe):
                def emit(k, r):
                    for s, b in steps_at(k, r, 2, ND4):
                        P = rows4(s)
                        pe.wait_ge(y_in.sem(b), y_in.at(s, b))
                        if begun(s - 1):
                            pe.wait_ge(p_a.sem, p_a.at(s - 1))
                        for j in range(J4):
                            last = pe.transpose(bank[0][:, j * P:(j + 1) * P], xyb[0:P, b, j, F:2 * F],
                                                ident[0:P, 0:P])
                        last.then_inc(p_t.sem, 1)
                    for s, b in steps_at(k, r, 3, ND4):
                        P = rows4(s)
                        pe.wait_ge(p_a.sem, p_a.at(s))
                        if begun(s - 1):
                            pe.wait_ge(p_z.sem, p_z.at(s - 1))
                        pe.matmul(bank[1][:, 0:J4 * P], w2[:, :], a1[:, b % 2, 0:J4 * P],
                                  start=True, stop=True).then_inc(p_y.sem, 1)
                    for s, b in steps_at(k, r, 4, ND4):
                        P = rows4(s)
                        pe.wait_ge(p_z.sem, p_z.at(s))
                        if begun(s - 1):
                            pe.wait_ge(p_x.sem, p_x.at(s - 1))
                        for j in range(J4):
                            last = pe.transpose(bank[2][0:P, j * F:(j + 1) * F], z2[:, b % 2, j * P:(j + 1) * P],
                                                ident[:, :])
                        last.then_inc(p_b.sem, 1)
                return emit

            LAG = 7
            DY = L[:, :, 0:2, :, :].rearrange("p b i j f -> p b (i j f)").rearrange("p b (j c) -> p b j c", j=J)
            E0, E1, E2, E3, E4 = bank[3], bank[4], bank[5], bank[6], bank[7]
            idx_ready.open(1), gathered.open(2 * J), fetched.open(1), turned.open(1), turned_sb.open(1), prod_ps.open(1)
            turned2_sb.open(1), hid_ps.open(1), prod_sb.open(2), ln_made.open(4), rooted.open(1), h_made.open(1), msg_made.open(1)
            same_made.open(1), sum_ps.open(J), carried.open(J), sum_sb.open(1), turned_b.open(1), turned_b_sb.open(1)
            prod_b_ps.open(1), prod_b_sb.open(1), stored.open(1)
            x4_v = by_step(x4_d)
            bothT = haT
            zT = hid[:, :, :, :].rearrange("p b m w -> p b (m w)")

            def l3_dve(dve):
                def emit(k, r):
                    for s, b in steps_at(k, r, 0, NS):
                        if begun(s - UNROLL):
                            dve.wait_ge(gathered.sem(b), gathered.at(s - UNROLL, b))
                        dve.sem_inc(dve_fence, 1)
                        dve.tensor_copy(idx[:, b, :], by_s.other[:, bass.ds(J * s, J)]).then_inc(idx_ready.sem, 1)
                    for s, b in steps_at(k, r, 5, NS):
                        dve.wait_ge(prod_sb.sem, prod_sb.at(s))
                        if begun(s - 2):
                            dve.wait_ge(h_made.sem, h_made.at(s - 2))
                        ln_stats(dve, ln_made, s, GX[:, b, :, 0:F], est[0][:, b % 2], emv[0][:, b % 2], 128, J, 0)
                    for s, b in steps_at(k, r, 6, NS):
                        build_same(dve, s, b)
                    for s, b in steps_at(k, r, 4, NS):
                        dve.wait_ge(hid_ps.sem, hid_ps.at(s))
                        dve.tensor_tensor(GX[:, b, :, 0:F], GX[:, b, :, 0:F], jview(E2[:, 0:W]), ALU.add) \
                            .then_inc(prod_sb.sem, 1)
                        if begun(s - 4):
                            dve.wait_ge(stored.sem(b), stored.at(s - 4, b))
                        dve.tensor_tensor(OUT[:, b], DY[:, b, :, 0:F], jview(E2[:, W:2 * W]), ALU.add) \
                            .then_inc(prod_sb.sem, 1)
                    for s, b in steps_at(k, r, 5, NS):
                        ln_scale(dve, ln_made, rooted, s, emv[0][:, b % 2], ers[0][:, b % 2], enm[0][:, b % 2], 128, 0)
                    for s, b in steps_at(k, r, 5, NS):
                        dve.wait_ge(h_made.sem, h_made.at(s))
                        if begun(s - 2):
                            dve.wait_ge(sum_ps.sem, sum_ps.at(s - 2))
                        if begun(s - 2):
                            dve.wait_ge(carried.sem, carried.at(s - 2))
                        dve.tensor_tensor(M[:, b % 2, :, 0:F], h[:, b % 2],
                                          by_s.w[:, bass.ds(J * s, J)].unsqueeze(2).to_broadcast([128, J, F]), ALU.mult) \
                            .then_inc(msg_made.sem, 1)
                    for s, b in steps_at(k, r, 6, NS):
                        sums_ready(dve, s)
                        if begun(s - 2):
                            dve.wait_ge(turned_b.sem, turned_b.at(s - 2))
                        dve.tensor_copy(hb[:, b % 2], SS4[:, :, 0:F]).then_inc(sum_sb.sem, 1)
                    for s, b in steps_at(k, r, 7, NS):
                        dve.wait_ge(prod_b_ps.sem, prod_b_ps.at(s))
                        dve.tensor_tensor(OUT[:, b], OUT[:, b], jview(E3[:, W:2 * W]), ALU.add) \
                            .then_inc(prod_b_sb.sem, 1)
                return emit

            def l3_pool(pool):
                def emit(k, r):
                    for s, b in steps_at(k, r, 1, NS):
                        pool.wait_ge(idx_ready.sem, idx_ready.at(s))
                        pool.sem_inc(pool_fence, 1)
                        if begun(s - 4):
                            pool.wait_ge(h_made.sem, h_made.at(s - 4))
                            pool.sem_inc(pool_fence, 1)
                        for table, half in ((x2_d, slice(0, F)), (y_d, slice(F, 2 * F))):
                            for j in range(J):
                                pool.indirect_dma_start(GX[:, b, j, half], None, table,
                                                        bass.IndirectOffsetOnAxis(ap=idx[:, b, j:j + 1], axis=0)) \
                                    .then_inc(gathered.sem(b), 16)
                return emit

            def l3_sp(sp):
                def emit(k, r):
                    for s, b in steps_at(k, r, 1, NS):
                        if begun(s - 4):
                            sp.wait_ge(prod_sb.sem, prod_sb.at(s - 4))
                            sp.sem_inc(sp_fence, 1)
                        sp.dma_start(DY[:, b], xyd_v[s]).then_inc(fetched.sem(b), 16)
                    for s, b in steps_at(k, r, 7, NS):
                        sp.wait_ge(prod_b_sb.sem, prod_b_sb.at(s))
                        sp.sem_inc(sp_fence, 1)
                        sp.dma_start(x4_v[s], OUT[:, b]).then_inc(stored.sem(b), 16)
                return emit

            def l3_act(act):
                def emit(k, r):
                    for s, b in steps_at(k, r, 5, NS):
                        root(act, ln_made, rooted, s, emv[0][:, b % 2], ers[0][:, b % 2], 128, 0)
                    for s, b in steps_at(k, r, 2, NS):
                        act.wait_ge(turned.sem, turned.at(s))
                        if begun(s - 2):
                            act.wait_ge(prod_ps.sem, prod_ps.at(s - 2))
                        act.activation(bothT[:, b % 2, :], E0[:, :], ACT.Relu, bias=bn[:, 1:2], scale=bn[:, 0:1]) \
                            .then_inc(turned_sb.sem, 1)
                    for s, b in steps_at(k, r, 6, NS):
                        carry(act, s, b, F, range(J - 1))
                    for s, b in steps_at(k, r, 5, NS):
                        act.wait_ge(ln_made.sem, ln_made.at(s))
                        if begun(s - 2):
                            act.wait_ge(msg_made.sem, msg_made.at(s - 2))
                        relu_norm(act, h_made, h[:, b % 2], GX[:, b, :, 0:F], ers[0][:, b % 2], enm[0][:, b % 2],
                                  128, J)
                    for s, b in steps_at(k, r, 3, NS):
                        act.wait_ge(prod_ps.sem, prod_ps.at(s))
                        if begun(s - 2):
                            act.wait_ge(hid_ps.sem, hid_ps.at(s - 2))
                        act.activation(zT[:, b % 2, :], E1[:, :], ACT.Relu, bias=bn[:, 3:4], scale=bn[:, 2:3]) \
                            .then_inc(turned2_sb.sem, 1)
                    for s, b in steps_at(k, r, 7, NS):
                        act.wait_ge(turned_b.sem, turned_b.at(s))
                        if begun(s - 2):
                            act.wait_ge(prod_b_ps.sem, prod_b_ps.at(s - 2))
                        act.activation(hT[:, b % 2, :], E3[:, 0:W], ACT.Copy).then_inc(turned_b_sb.sem, 1)
                    for s, b in steps_at(k, r, 6, NS):
                        carry(act, s, b, F, range(J - 1, J))
                return emit

            def l3_pe(pe):
                def emit(k, r):
                    for s, b in steps_at(k, r, 2, NS):
                        pe.wait_ge(gathered.sem(b), gathered.at(s, b))
                        pe.wait_ge(fetched.sem(b), fetched.at(s, b))
                        if begun(s - 1):
                            pe.wait_ge(turned_sb.sem, turned_sb.at(s - 1))
                        for i, rows_ in enumerate((GX, DY)):
                            for j in range(J):
                                last = pe.transpose(E0[:, i * W + j * 128:i * W + (j + 1) * 128],
                                                    rows_[:, b, j, F:2 * F], ident[:, :])
                        last.then_inc(turned.sem, 1)
                    for s, b in steps_at(k, r, 7, NS):
                        pe.wait_ge(sum_sb.sem, sum_sb.at(s))
                        if begun(s - 1):
                            pe.wait_ge(prod_b_sb.sem, prod_b_sb.at(s - 1))
                        for j in range(J):
                            last = pe.transpose(E3[:, j * 128:(j + 1) * 128], hb[:, b % 2, j, :], ident[:, :])
                        last.then_inc(turned_b.sem, 1)
                    for s, b in steps_at(k, r, 4, NS):
                        pe.wait_ge(turned2_sb.sem, turned2_sb.at(s))
                        if begun(s - 1):
                            pe.wait_ge(prod_sb.sem, prod_sb.at(s - 1))
                        for i in range(2 * J):
                            last = pe.transpose(E2[:, i * 128:(i + 1) * 128], zT[:, b % 2, i * 128:(i + 1) * 128],
                                                ident[:, :])
                        last.then_inc(hid_ps.sem, 1)
                    for s, b in steps_at(k, r, 6, NS):
                        sum_segments(pe, s, b, F)
                    for s, b in steps_at(k, r, 3, NS):
                        pe.wait_ge(turned_sb.sem, turned_sb.at(s))
                        if begun(s - 1):
                            pe.wait_ge(turned2_sb.sem, turned2_sb.at(s - 1))
                        pe.matmul(E1[:, :], w2[:, :], bothT[:, b % 2, :], start=True, stop=True) \
                            .then_inc(prod_ps.sem, 1)
                    for s, b in steps_at(k, r, 7, NS):
                        pe.wait_ge(turned_b_sb.sem, turned_b_sb.at(s))
                        if begun(s - 1):
                            pe.wait_ge(prod_b_sb.sem, prod_b_sb.at(s - 1))
                        for j in range(J):
                            last = pe.matmul(E3[:, W + j * F:W + (j + 1) * F], hT[:, b % 2, j * 128:(j + 1) * 128],
                                             w3[:, :], start=True, stop=True)
                        last.then_inc(prod_b_ps.sem, 1)
                return emit

            makers = {
                "sync": (last_dense_sp, l3_sp), "vector": (last_dense_dve, l3_dve),
                "scalar": (last_dense_act, l3_act), "tensor": (last_dense_pe, l3_pe), "gpsimd": (None, l3_pool)}
            total = max(ND4 + 5, NS + LAG)

            def go(name, eng):
                dense_part, edge_part = makers[name]
                streams = []
                if dense_part:
                    streams.append((dense_part(eng), 0, (0, ND4 + 5), (3 * UNROLL, NF4)))
                streams.append((edge_part(eng), 0, (0, NS + LAG), (-(-(LAG + UNROLL) // UNROLL) * UNROLL, NS)))
                drive(eng, total, streams)
                if name == "sync":
                    all_stored(stored)(eng)
                    all_stored(x3_out, ND4)(eng)

            with nc.Block() as block:
                block.sync(lambda sp: go("sync", sp))
                block.gpsimd(lambda pool: go("gpsimd", pool))
                block.scalar(lambda act: go("scalar", act))
                block.vector(lambda dve: go("vector", dve))
                block.tensor(lambda pe: go("tensor", pe))
            idx_ready.close(NS), gathered.close(NS), fetched.close(NS), stored.close(NS)

        replace_rows(out, x4_v, OUT)


_PLAIN = ['x', 'L0_gnn_W1_l', 'L0_gnn_b1', 'L0_gnn_W1_r', 'L0_gnn_W2_l', 'L0_gnn_b2', 'L0_gnn_W2_r', 'L1_gnn_Wq',
          'L1_gnn_bq', 'L1_gnn_Wk', 'L1_gnn_bk', 'L1_gnn_We', 'L1_gnn_be', 'L1_gnn_Wv', 'L1_gnn_bv', 'L2_gnn_eps',
          'L2_gnn_w1', 'L2_gnn_b1', 'L2_gnn_gamma1', 'L2_gnn_beta1', 'L2_gnn_w2', 'L2_gnn_b2', 'L2_gnn_gamma2',
          'L2_gnn_beta2', 'L3_gnn_W']


def kernel(**inputs):
    import numpy as _np
    import concourse.bacc as _bacc
    from concourse import mybir as _mybir
    from concourse.bass_utils import run_bass_kernel_spmd as _run

    nc = _bacc.Bacc("TRN2", target_bir_lowering=False, num_devices=1)
    N, E = inputs['x'].shape[0], inputs['src'].shape[0]
    tiles = -(-E // EPT)
    tiles += tiles % J
    length = max(tiles * EPT + 2, -(-E // 128) * 128 + 1)
    arrays, args = {}, {}

    def give(name, a):
        arrays[f"in_{name}_dram"] = a
        args[name] = nc.dram_tensor(f"in_{name}_dram", a.shape, _mybir.dt.from_np(a.dtype), kind="ExternalInput").ap()

    for name in _PLAIN:
        give(name, _np.ascontiguousarray(inputs[name]))
    for name, before, after in (('src', 0, N), ('dst', -1, N), ('edge_weight', 0, 0), ('edge_weight1', 0, 0)):
        a = _np.asarray(inputs[name]).reshape(-1)
        padded = _np.full((length,), after, a.dtype)
        padded[0] = before
        padded[1:1 + E] = a
        give(name, padded)
    out = nc.dram_tensor("out_0_dram", [N, F], _mybir.dt.float32, kind="ExternalOutput").ap()
    gnn_kernel(nc, N, E, args, out)
    r = _run(nc, [arrays], core_ids=[0])
    return r.results[0]["out_0_dram"]
```
